# Optimizing a Trainium2 kernel written in Bass

```python
import numpy as np
import jax
import jax.numpy as jnp

def _softmax(x, axis=-1):
    return jax.nn.softmax(x, axis=axis)

def _gelu(x):
    return jax.nn.gelu(x, approximate=True)

def _silu(x):
    return jax.nn.silu(x)

def _sigmoid(x):
    return jax.nn.sigmoid(x)

def _layernorm(x, axis=-1, eps=1e-05):
    m = jnp.mean(x, axis=axis, keepdims=True)
    v = jnp.var(x, axis=axis, keepdims=True)
    return (x - m) / jnp.sqrt(v + eps)

def _scatter_add(tgt, idx, src, axis=0):
    return tgt.at[idx].add(src)

def _segment_sum(src, seg, n):
    return jax.ops.segment_sum(src, seg, n)
kernel_name = 'mk_decoder_postln_d1_seqx_r8_a6c339'

def setup_inputs(seed: int=0):
    np.random.seed(seed)
    _w = jnp.asarray

    def _rec_inputs():
        import jax
        import jax.numpy as jnp
        _rk = jax.random.key(seed)
        x = 7.22e-05 + 1 * jax.random.normal(jax.random.fold_in(_rk, 1), (16, 128, 128), jnp.float32)
        _lenS = 128 - jax.random.randint(jax.random.fold_in(_rk, 7), (16,), 0, max(1, 128 // 4) + 1, jnp.int32)
        _lenS2 = 128 - jax.random.randint(jax.random.fold_in(_rk, 8), (16,), 0, max(1, 128 // 4) + 1, jnp.int32)
        _ctx_1024P = jax.random.normal(jax.random.fold_in(_rk, 11), (16, 16, 128), jnp.float32)
        _ctx_1024c = jax.random.dirichlet(jax.random.fold_in(_rk, 511), 0.3 * jnp.ones((16,), jnp.float32), (16, 128))
        _ctx_1024t = jnp.einsum('bsk,bkd->bsd', _ctx_1024c, _ctx_1024P)
        _ctx_1024t = _ctx_1024t * jax.lax.rsqrt(jnp.mean(jnp.square(_ctx_1024t)) + 1e-12) * 0.953939
        ctx_1024 = 4.13588e-05 + 0.999923 * (_ctx_1024t + 0.3 * jax.random.normal(jax.random.fold_in(_rk, 611), (16, 128, 128), jnp.float32))
        _validS = jnp.arange(128)[None, :] < _lenS[:, None]
        _validS2 = jnp.arange(128)[None, :] < _lenS2[:, None]
        _causal = jnp.tril(jnp.ones((128, 128), dtype=bool))
        mask_SxS2_fk0 = jnp.where(jnp.broadcast_to(_validS2[0:1, :], (128, 128)), -1000000000.0, 0.0).astype(jnp.float32)
        return (x, ctx_1024, mask_SxS2_fk0)
    x, ctx_1024, mask_SxS2_fk0 = _rec_inputs()

    def _L0_attn_setup():
        import jax, jax.numpy as jnp
        import numpy as np
        N_HEADS = 16
        WINDOW = 128
        EPS = 1e-06

        def rmsnorm(x, w):
            return x * jax.lax.rsqrt(jnp.mean(x * x, axis=-1, keepdims=True) + EPS) * w

        def linear(x, W, b=None):
            y = jnp.einsum('bsd,od->bso', x, W)
            return y + b if b is not None else y

        def min_gru(x, Wg, bg, Wv, bv, Wd, bd):
            g = linear(x, Wg, bg)
            v = linear(x, Wv, bv)
            d = linear(x, Wd, bd)
            x_scan = jax.nn.sigmoid(g) * jnp.tanh(v)
            a = 0.001 + 0.998 * jax.nn.sigmoid(d)

            def comb(e1, e2):
                a1, x1 = e1
                a2, x2 = e2
                return (a1 * a2, a2 * x1 + x2)
            _, h = jax.lax.associative_scan(comb, (a, x_scan), axis=1)
            return h

        def sliding_attn(x, Wqkv, Wo):
            B, S, D = x.shape
            Hh, Wd_ = (N_HEADS, D // N_HEADS)
            W = WINDOW
            qkv = linear(x, Wqkv).reshape(B, S, 3, Hh, Wd_)
            q = qkv[:, :, 0].transpose(0, 2, 1, 3)
            k = qkv[:, :, 1].transpose(0, 2, 1, 3)
            v = qkv[:, :, 2].transpose(0, 2, 1, 3)
            nC = S // W
            qc = q.reshape(B, Hh, nC, W, Wd_)
            kc = k.reshape(B, Hh, nC, W, Wd_)
            vc = v.reshape(B, Hh, nC, W, Wd_)
            kp = jnp.concatenate([jnp.zeros_like(kc[:, :, :1]), kc[:, :, :-1]], axis=2)
            vp = jnp.concatenate([jnp.zeros_like(vc[:, :, :1]), vc[:, :, :-1]], axis=2)
            kk = jnp.concatenate([kp, kc], axis=3)
            vv = jnp.concatenate([vp, vc], axis=3)
            scores = jnp.einsum('bhcqd,bhckd->bhcqk', qc, kk) / np.sqrt(Wd_)
            j = jnp.arange(W)[:, None]
            kidx = jnp.arange(2 * W)[None, :]
            cidx = jnp.arange(nC)[:, None, None]
            mask = (kidx <= W + j) & (kidx >= j + 1) & ((kidx >= W) | (cidx > 0))
            scores = jnp.where(mask[None, None], scores, jnp.finfo(scores.dtype).min)
            attn = jax.nn.softmax(scores, axis=-1)
            out = jnp.einsum('bhcqk,bhckd->bhcqd', attn, vv)
            out = out.reshape(B, Hh, S, Wd_).transpose(0, 2, 1, 3).reshape(B, S, D)
            return linear(out, Wo)

        def glu_ffn(x, Wgate, Wup, Wout):
            return linear(jax.nn.silu(linear(x, Wgate)) * linear(x, Wup), Wout)
        key = jax.random.key(seed)
        B, S, D, DFF = (4, 256, 128, 512)
        ks = jax.random.split(key, 10)
        w = lambda k, shp: jax.random.normal(k, shp, dtype=jnp.float32) * 0.02
        return {'x': jax.random.normal(ks[0], (B, S, D), dtype=jnp.float32), 'w_rms_mix': jnp.ones((D,), jnp.float32), 'Wg': w(ks[1], (D, D)), 'bg': jnp.zeros((D,), jnp.float32), 'Wv': w(ks[2], (D, D)), 'bv': jnp.zeros((D,), jnp.float32), 'Wd': w(ks[3], (D, D)), 'bd': jnp.ones((D,), jnp.float32), 'w_rms_attn': jnp.ones((D,), jnp.float32), 'Wqkv': w(ks[4], (3 * D, D)), 'Wo': w(ks[5], (D, D)), 'w_rms_ffn': jnp.ones((D,), jnp.float32), 'Wgate': w(ks[6], (DFF, D)), 'Wup': w(ks[7], (DFF, D)), 'Wout': w(ks[8], (D, DFF))}
    _L0_attn_all = _L0_attn_setup()
    _L0_attn_in = {k: v for k, v in _L0_attn_all.items() if k in ('w_rms_mix', 'Wg', 'bg', 'Wv', 'bv', 'Wd', 'bd', 'w_rms_attn', 'Wqkv', 'Wo', 'w_rms_ffn', 'Wgate', 'Wup', 'Wout')}
    del _L0_attn_all

    def _L0_xattn_setup():
        import jax, jax.numpy as jnp
        import numpy as np
        M = 128
        N = 128
        B, S = (4, 256)
        key = jax.random.key(seed)
        ks = jax.random.split(key, 7)
        scale = 1.0 / np.sqrt(M)
        q = jax.random.normal(ks[0], (B, S, M), dtype=jnp.float32)
        k = jax.random.normal(ks[1], (B, S, M), dtype=jnp.float32)
        v = jax.random.normal(ks[2], (B, S, N), dtype=jnp.float32)
        causal = jnp.tril(jnp.ones((S, S), dtype=bool))
        attn_mask = jnp.where(causal, 0.0, -1000000000.0).astype(jnp.float32)
        Wq = jax.random.normal(ks[3], (N, M), dtype=jnp.float32) * scale
        Wk = jax.random.normal(ks[4], (N, M), dtype=jnp.float32) * scale
        Wv = jax.random.normal(ks[5], (N, N), dtype=jnp.float32) * scale
        bv = jax.random.normal(ks[6], (N,), dtype=jnp.float32) * scale
        return {'q': q, 'k': k, 'v': v, 'attn_mask': attn_mask, 'Wq': Wq, 'Wk': Wk, 'Wv': Wv, 'bv': bv}
    _L0_xattn_all = _L0_xattn_setup()
    _L0_xattn_in = {k: v for k, v in _L0_xattn_all.items() if k in ('Wq', 'Wk', 'Wv', 'bv')}
    del _L0_xattn_all

    def _L0_ffn_setup():
        import jax, jax.numpy as jnp
        import numpy as np
        B, S, D, H, DOUT, E, K = (4, 256, 128, 128, 128, 8, 2)
        key = jax.random.key(seed)
        k1, k2, k3, k4 = jax.random.split(key, 4)
        x = jax.random.normal(k1, (B, S, D), dtype=jnp.float32)
        Wr = jax.random.normal(k2, (D, E), dtype=jnp.float32) * 0.02
        Wi = jax.random.normal(k3, (E, D, H), dtype=jnp.float32) * 0.02
        Wo = jax.random.normal(k4, (E, H, DOUT), dtype=jnp.float32) * 0.02
        return {'x': x, 'Wr': Wr, 'Wi': Wi, 'Wo': Wo}
    _L0_ffn_all = _L0_ffn_setup()
    _L0_ffn_in = {k: v for k, v in _L0_ffn_all.items() if k in ('Wr', 'Wi', 'Wo')}
    del _L0_ffn_all
    return {'x': x, 'ctx_1024': ctx_1024, 'mask_SxS2_fk0': mask_SxS2_fk0, 'L0_attn_w_rms_mix': _L0_attn_in['w_rms_mix'], 'L0_attn_Wg': _L0_attn_in['Wg'], 'L0_attn_bg': _L0_attn_in['bg'], 'L0_attn_Wv': _L0_attn_in['Wv'], 'L0_attn_bv': _L0_attn_in['bv'], 'L0_attn_Wd': _L0_attn_in['Wd'], 'L0_attn_bd': _L0_attn_in['bd'], 'L0_attn_w_rms_attn': _L0_attn_in['w_rms_attn'], 'L0_attn_Wqkv': _L0_attn_in['Wqkv'], 'L0_attn_Wo': _L0_attn_in['Wo'], 'L0_attn_w_rms_ffn': _L0_attn_in['w_rms_ffn'], 'L0_attn_Wgate': _L0_attn_in['Wgate'], 'L0_attn_Wup': _L0_attn_in['Wup'], 'L0_attn_Wout': _L0_attn_in['Wout'], 'L0_xattn_Wq': _L0_xattn_in['Wq'], 'L0_xattn_Wk': _L0_xattn_in['Wk'], 'L0_xattn_Wv': _L0_xattn_in['Wv'], 'L0_xattn_bv': _L0_xattn_in['bv'], 'L0_ffn_Wr': _L0_ffn_in['Wr'], 'L0_ffn_Wi': _L0_ffn_in['Wi'], 'L0_ffn_Wo': _L0_ffn_in['Wo']}

def reference(x, ctx_1024, mask_SxS2_fk0, L0_attn_w_rms_mix, L0_attn_Wg, L0_attn_bg, L0_attn_Wv, L0_attn_bv, L0_attn_Wd, L0_attn_bd, L0_attn_w_rms_attn, L0_attn_Wqkv, L0_attn_Wo, L0_attn_w_rms_ffn, L0_attn_Wgate, L0_attn_Wup, L0_attn_Wout, L0_xattn_Wq, L0_xattn_Wk, L0_xattn_Wv, L0_xattn_bv, L0_ffn_Wr, L0_ffn_Wi, L0_ffn_Wo):
    import jax
    import jax.numpy as jnp

    def _L0_attn_ref(x, w_rms_mix, Wg, bg, Wv, bv, Wd, bd, w_rms_attn, Wqkv, Wo, w_rms_ffn, Wgate, Wup, Wout):
        import jax, jax.numpy as jnp
        import numpy as np
        N_HEADS = 16
        WINDOW = 128
        EPS = 1e-06

        def rmsnorm(x, w):
            return x * jax.lax.rsqrt(jnp.mean(x * x, axis=-1, keepdims=True) + EPS) * w

        def linear(x, W, b=None):
            y = jnp.einsum('bsd,od->bso', x, W)
            return y + b if b is not None else y

        def min_gru(x, Wg, bg, Wv, bv, Wd, bd):
            g = linear(x, Wg, bg)
            v = linear(x, Wv, bv)
            d = linear(x, Wd, bd)
            x_scan = jax.nn.sigmoid(g) * jnp.tanh(v)
            a = 0.001 + 0.998 * jax.nn.sigmoid(d)

            def comb(e1, e2):
                a1, x1 = e1
                a2, x2 = e2
                return (a1 * a2, a2 * x1 + x2)
            _, h = jax.lax.associative_scan(comb, (a, x_scan), axis=1)
            return h

        def sliding_attn(x, Wqkv, Wo):
            B, S, D = x.shape
            Hh, Wd_ = (N_HEADS, D // N_HEADS)
            W = WINDOW
            qkv = linear(x, Wqkv).reshape(B, S, 3, Hh, Wd_)
            q = qkv[:, :, 0].transpose(0, 2, 1, 3)
            k = qkv[:, :, 1].transpose(0, 2, 1, 3)
            v = qkv[:, :, 2].transpose(0, 2, 1, 3)
            nC = S // W
            qc = q.reshape(B, Hh, nC, W, Wd_)
            kc = k.reshape(B, Hh, nC, W, Wd_)
            vc = v.reshape(B, Hh, nC, W, Wd_)
            kp = jnp.concatenate([jnp.zeros_like(kc[:, :, :1]), kc[:, :, :-1]], axis=2)
            vp = jnp.concatenate([jnp.zeros_like(vc[:, :, :1]), vc[:, :, :-1]], axis=2)
            kk = jnp.concatenate([kp, kc], axis=3)
            vv = jnp.concatenate([vp, vc], axis=3)
            scores = jnp.einsum('bhcqd,bhckd->bhcqk', qc, kk) / np.sqrt(Wd_)
            j = jnp.arange(W)[:, None]
            kidx = jnp.arange(2 * W)[None, :]
            cidx = jnp.arange(nC)[:, None, None]
            mask = (kidx <= W + j) & (kidx >= j + 1) & ((kidx >= W) | (cidx > 0))
            scores = jnp.where(mask[None, None], scores, jnp.finfo(scores.dtype).min)
            attn = jax.nn.softmax(scores, axis=-1)
            out = jnp.einsum('bhcqk,bhckd->bhcqd', attn, vv)
            out = out.reshape(B, Hh, S, Wd_).transpose(0, 2, 1, 3).reshape(B, S, D)
            return linear(out, Wo)

        def glu_ffn(x, Wgate, Wup, Wout):
            return linear(jax.nn.silu(linear(x, Wgate)) * linear(x, Wup), Wout)
        x = x + min_gru(rmsnorm(x, w_rms_mix), Wg, bg, Wv, bv, Wd, bd)
        x = x + sliding_attn(rmsnorm(x, w_rms_attn), Wqkv, Wo)
        x = x + glu_ffn(rmsnorm(x, w_rms_ffn), Wgate, Wup, Wout)
        return x

    def _L0_xattn_ref(q, k, v, attn_mask, Wq, Wk, Wv, bv):
        import jax, jax.numpy as jnp
        import numpy as np
        M = 128
        N = 128
        B, S = (4, 256)
        qp = jnp.einsum('bsm,nm->bsn', q, Wq)
        kp = jnp.einsum('bsm,nm->bsn', k, Wk)
        vp = jnp.einsum('bsn,on->bso', v, Wv) + bv
        scores = jnp.einsum('bqn,bkn->bqk', qp, kp) / jnp.sqrt(jnp.float32(N))
        scores = scores + attn_mask
        w = jax.nn.softmax(scores, axis=-1)
        return jnp.einsum('bqk,bkn->bqn', w, vp)

    def _L0_ffn_ref(x, Wr, Wi, Wo):
        import jax, jax.numpy as jnp
        import numpy as np
        B, S, D, H, DOUT, E, K = (4, 256, 128, 128, 128, 8, 2)
        b, s, d = x.shape
        e_cnt, _, h = Wi.shape
        dout = Wo.shape[2]
        xf = x.reshape(-1, d)
        T = xf.shape[0]
        probs = jax.nn.softmax(xf @ Wr, axis=-1)
        topk_p, topk_i = jax.lax.top_k(probs, K)
        mask = topk_i[:, :, None] == jnp.arange(e_cnt)[None, None, :]
        hmix = jnp.zeros((T, K, h), dtype=xf.dtype)
        for e in range(e_cnt):
            he = xf @ Wi[e]
            hmix = hmix + jnp.where(mask[:, :, e][:, :, None], he[:, None, :], 0.0)
        o = jnp.zeros((T, K, dout), dtype=xf.dtype)
        for e in range(e_cnt):
            oe = jnp.einsum('tkh,hd->tkd', hmix, Wo[e])
            o = o + jnp.where(mask[:, :, e][:, :, None], oe, 0.0)
        out = jnp.sum(o * topk_p[:, :, None], axis=1)
        return out.reshape(b, s, dout)
    x = _layernorm(x + _L0_attn_ref(x, L0_attn_w_rms_mix, L0_attn_Wg, L0_attn_bg, L0_attn_Wv, L0_attn_bv, L0_attn_Wd, L0_attn_bd, L0_attn_w_rms_attn, L0_attn_Wqkv, L0_attn_Wo, L0_attn_w_rms_ffn, L0_attn_Wgate, L0_attn_Wup, L0_attn_Wout), axis=-1)
    x = _layernorm(x + _L0_xattn_ref(x, ctx_1024, ctx_1024, mask_SxS2_fk0, L0_xattn_Wq, L0_xattn_Wk, L0_xattn_Wv, L0_xattn_bv), axis=-1)
    x = _layernorm(x + _L0_ffn_ref(x, L0_ffn_Wr, L0_ffn_Wi, L0_ffn_Wo), axis=-1)
    return x

_drawn_inputs = setup_inputs


def setup_inputs(seed=0):
    import zlib

    import numpy as np

    out = dict(_drawn_inputs(seed))
    spreads = {'mask_SxS2_fk0': (-1000000000.0, 0.2),
     'L0_attn_w_rms_mix': (1.0, 0.6),
     'L0_attn_bg': (0.0, 0.8),
     'L0_attn_bv': (0.0, 0.1),
     'L0_attn_bd': (1.0, 0.6),
     'L0_attn_w_rms_attn': (1.0, 0.6),
     'L0_attn_w_rms_ffn': (1.0, 0.6)}
    factors = {'L0_attn_Wg': 7.584,
     'L0_attn_Wd': 8.0,
     'L0_attn_Wqkv': 8.0,
     'L0_attn_Wo': 8.0,
     'L0_attn_Wgate': 8.0,
     'L0_attn_Wup': 8.0,
     'L0_attn_Wout': 8.0,
     'L0_ffn_Wr': 5.622,
     'L0_ffn_Wi': 4.876,
     'L0_ffn_Wo': 4.857}
    for name, (base, spread) in spreads.items():
        noise = np.random.default_rng([zlib.crc32(name.encode()), seed]).standard_normal(out[name].shape)
        drawn = base * np.exp(spread * noise) if base else spread * noise
        out[name] = jnp.asarray(drawn.astype(out[name].dtype))
    for name, factor in factors.items():
        out[name] = (out[name] * factor).astype(out[name].dtype)
    return out
```

```python
from contextlib import ExitStack

import concourse.bass as bass
from concourse import mybir

P = 128
HEADS = 16
HD = P // HEADS
EXPERTS = 8
FF = 4
PARTS = 3
PAIRS = PARTS * PARTS
QROWS = PAIRS * HD
SROWS = QROWS + PARTS
QDUP = PARTS + PARTS - 1
QUARTER = HEADS // 4
RMS_EPS = 1e-6
LN_EPS = 1e-5
MASKED = -1e30

GRU, QKV, MAX, ATT, FFN, XAT, MOE = range(7)
STAGES = 7

ALU = mybir.AluOpType
ACT = mybir.ActivationFunctionType
F32 = mybir.dt.float32
BF16 = mybir.dt.bfloat16
AX_X = mybir.AxisListType.X

TILE_SEMS = """
gru_ss gru_ms gru_rs gru_xn gru_xT_ps gru_xT gru_gates_ps gru_tanh gru_xs gru_decay gru_scan gru_hT_ps gru_x1
qkv_ss qkv_ms qkv_rs qkv_xn qkv_xT_ps qkv_xT qkv_ps qkv_hi qkv_rest qkv_mid qkv_lo
max_scores_ps max_max max_n1 max_r1 max_n2 max_n3 max_mT_ps max_mT max_v_ps max_v
att_scores_ps att_p att_o_ps att_rd att_o att_oT_ps att_oT att_y_ps att_x2
ffn_ss ffn_ms ffn_rs ffn_xn ffn_xT_ps ffn_xT ffn_gu_ps ffn_tanh ffn_t1 ffn_h ffn_x02 ffn_y_ps ffn_z
ffn_stats ffn_mv ffn_ve ffn_rs1 ffn_y1 ctx_T_ps ctx_T ctx_kv_ps ctx_kv
xat_xT_ps xat_xT xat_s_ps xat_sm xat_negm xat_p xat_pT_ps xat_pT xat_rd xat_y1b xat_y_ps xat_z
xat_stats xat_mv xat_ve xat_rs xat_y2
moe_xT_ps moe_xT moe_logits_ps moe_top moe_negm moe_e moe_gt moe_eq moe_cum moe_lt moe_both moe_sel moe_rd moe_c moe_lg
moe_m_ps moe_acc moe_z moe_stats moe_mv moe_ve moe_rs moe_out
""".split()
DMA_SEMS = "x_in ctx_in w_in_a w_in_b w_in_c q_saved q_stacked k_stacked m_stacked stored".split()
SETUP_SEMS = "const_pool const_dve w_ps w_dve w_act".split()


def decoder_layer(nc, x, ctx, mask, w_mix, Wg, bg, Wv, bv, Wd, bd, w_attn, Wqkv, Wo, w_ffn, Wgate, Wup,
                  Wout, xWq, xWk, xWv, xbv, Wr, Wi, Wmo, out):
    TILES = x.shape[0]
    LAST = TILES + STAGES - 1
    LOOP = STAGES + STAGES % 2
    assert TILES % 2 == 0 and TILES > LOOP and x.shape[1:] == (P, P)

    with ExitStack() as stack:
        def sb(name, shape, dt=F32):
            return stack.enter_context(nc.sbuf_tensor(name, shape, dt))

        def psum(name, shape, dt=F32):
            return stack.enter_context(nc.psum_tensor(name, shape, dt))

        S = {name: stack.enter_context(nc.semaphore(name)) for name in TILE_SEMS + DMA_SEMS + SETUP_SEMS}

        ps_scores = psum("ps_scores", [P, QUARTER, P])
        ps_probs = psum("ps_probs", [P, QUARTER, P])
        ps_wide = psum("ps_wide", [P, 2, FF * P])
        ps_turn0 = psum("ps_turn0", [P, 4, P])
        ps_turn1 = psum("ps_turn1", [P, 4, P])
        ps_proj = psum("ps_proj", [P, 4, P])
        ps_sum = psum("ps_sum", [P, 4, P])
        turn = [ps_turn0[:, 0, :], ps_turn1[:, 0, :]]
        ps_logits = ps_turn1[:, 1, 0:EXPERTS]
        ps_mT = ps_turn1[:, 2, 0:P // 2].bitcast(BF16)
        proj = ps_proj[:, 0:3, :]
        ps_y = ps_sum[:, 0, :]
        ps_o = ps_sum[:, 1:4, :].rearrange("p a b -> p (a b)")[:, 0:HEADS * (HD + 1)].rearrange("p (h e) -> p h e", h=HEADS)

        ident = sb("ident", [P, P])
        identb = sb("identb", [P, P], BF16)
        above = sb("above", [P, 4, P], BF16)
        below = sb("below", [P, 4, P], BF16)
        neghalf = sb("neghalf", [P, 1])
        ones8 = sb("ones8", [P, EXPERTS])
        mask_sb = sb("mask_sb", [P, P])
        xbv_sb = sb("xbv_sb", [P, P])
        cols = sb("cols", [P, 6])
        half_b = sb("half_b", [P, 2])
        NRAW = 28
        raw = sb("raw", [P, NRAW, P])
        R_GRU, R_WO, R_QKV, R_XWV, R_GATE, R_UP, R_OUT, R_WI = 0, 3, 4, 7, 8, 12, 16, 20
        raw_xq = sb("raw_xq", [P, P])
        raw_xk = sb("raw_xk", [P, P])
        wr_sb = sb("wr_sb", [P, EXPERTS])
        wmo_sb = sb("wmo_sb", [P, EXPERTS, P])
        gruT = sb("gruT", [P, 3, P])
        woT = sb("woT", [P, P])
        qkvT = sb("qkvT", [P, 3, P])
        xwvT = sb("xwvT", [P, P])
        guT = sb("guT", [P, 2, FF * P])
        outT = sb("outT", [P, FF, P])
        wiT = sb("wiT", [P, EXPERTS, P])
        w_kq = sb("w_kq", [P, P])
        w_moe = sb("w_moe", [P, EXPERTS, P])

        x_all = sb("x_all", [P, TILES, P])
        x1_all = sb("x1_all", [P, TILES, P])
        junk = sb("junk", [P, 3, P])
        ss = sb("ss", [P, 3])
        ms = sb("ms", [P, 3])
        rs = sb("rs", [P, 3])
        xn = sb("xn", [P, 3, P])
        xT = sb("xT", [P, 2, P])
        qkv_xT = sb("qkv_xT", [P, 2, P])
        gru_t = sb("gru_t", [P, 3, P])
        gru_xs = sb("gru_xs", [P, P])
        gru_a = sb("gru_a", [P, P])
        gru_h = sb("gru_h", [P, P])
        qk_rest = sb("qk_rest", [P, 2, P])
        qk_parts = sb("qk_parts", [P, 2, PARTS, P], BF16)
        q_stack = sb("q_stack", [P, 2, HEADS, P], BF16)
        k_stack = sb("k_stack", [P, 2, HEADS, P], BF16)
        neg_max = sb("neg_max", [P, HEADS])
        nm_rest = sb("nm_rest", [P, HEADS])
        nm_parts = sb("nm_parts", [P, PARTS, HEADS], BF16)
        nmT = sb("nmT", [PARTS * HEADS, P], BF16)
        values = sb("values", [P, 2, HEADS, HD + 1])
        probs = sb("probs", [P, 4, QUARTER, P])
        att_rd = sb("att_rd", [P, HEADS])
        att_o = sb("att_o", [P, P])
        att_oT = sb("att_oT", [P, P])
        x2 = sb("x2", [P, 2, P])
        x02 = sb("x02", [P, P])
        gate_t = sb("gate_t", [P, FF * P])
        gate_1 = sb("gate_1", [P, FF * P])
        hidden = sb("hidden", [P, FF, P])
        z = sb("z", [P, 3, P])
        stats = sb("stats", [P, 3, 6])
        mv = sb("mv", [P, 3, 2])
        ve = sb("ve", [P, 3])
        lrs = sb("lrs", [P, 3])
        y1 = sb("y1", [P, 2, P])
        ctx_sb = sb("ctx_sb", [P, 2, P])
        ctxT = sb("ctxT", [P, P])
        ctx_kv = sb("ctx_kv", [P, 2, 2, P])
        y1T = sb("y1T", [P, P])
        xat_s = sb("xat_s", [P, P])
        xat_m = sb("xat_m", [P, 2])
        xat_p = sb("xat_p", [P, P])
        xat_l = sb("xat_l", [P, 2])
        xat_pT = sb("xat_pT", [P, P])
        y1b = sb("y1b", [P, P])
        y2 = sb("y2", [P, 2, P])
        y2T = sb("y2T", [P, P])
        top = sb("top", [P, EXPERTS])
        moe_lg = sb("moe_lg", [P, EXPERTS])
        moe_m = sb("moe_m", [P, 2])
        moe_e = sb("moe_e", [P, EXPERTS])
        moe_l = sb("moe_l", [P, 2])
        moe_gt = sb("moe_gt", [P, EXPERTS])
        moe_n = sb("moe_n", [P, 1])
        moe_eq = sb("moe_eq", [P, EXPERTS])
        moe_cum = sb("moe_cum", [P, EXPERTS])
        moe_lt = sb("moe_lt", [P, EXPERTS])
        moe_both = sb("moe_both", [P, EXPERTS])
        moe_sel = sb("moe_sel", [P, EXPERTS])
        moe_c = sb("moe_c", [P, EXPERTS])
        acc = sb("acc", [P, 2, P])
        out_sb = sb("out_sb", [P, 2, P])
        scratch = nc.dram_tensor("qk_scratch", [2, QDUP + PARTS, P, P], BF16).ap()

        def after(eng, name, n, alone=False):
            if isinstance(n, int) and n <= 0:
                return
            if alone and not isinstance(n, int):
                eng.lower_val(n)
                eng.wait_ge(S["const_pool"], 8)
            eng.wait_ge(S[name], n)

        def tile_at(t, parity, stage):
            k = t - stage
            if isinstance(t, int) and not 0 <= k < TILES:
                return None
            return k, (parity + stage) % 2

        def steps(eng, step):
            for t in range(LOOP):
                step(t, t % 2)
            with eng.Fori(LOOP, TILES - 1, 2) as i:
                step(i, 0)
                step(i + 1, 1)
            for t in range(TILES, LAST):
                step(t, t % 2)

        TURN0 = [(XAT, "xat_xT"), (GRU, "gru_xT"), (FFN, "ffn_xT"), (XAT, "xat_pT"), (FFN, "ctx_T")]
        TURN1 = [(MOE, "moe_xT"), (QKV, "qkv_xT"), (MOE, "moe_lg"), (GRU, "gru_x1"), (ATT, "att_oT"), (MAX, "max_mT")]
        PROJ = [(GRU, "gru_tanh"), (MAX, "max_v"), (QKV, "qkv_rest"), (FFN, "ctx_kv")]
        SUM = [(XAT, "xat_sm"), (ATT, "att_o"), (ATT, "att_x2"), (XAT, "xat_z"), (FFN, "ffn_z")]
        WIDE = [(MOE, "moe_z"), (FFN, "ffn_h")]

        def region_free(eng, users, t, me):
            for back in range(1, len(users) + 1):
                n = me - back
                stage, name = users[n]
                k = t - stage - (1 if n < 0 else 0)
                if isinstance(k, int) and not 0 <= k < TILES:
                    continue
                after(eng, name, k + 1)
                return

        block = stack.enter_context(nc.Block())

        @block.sync
        def _(sp):
            for n, v in enumerate((w_mix, w_attn, w_ffn, bg, bv, bd)):
                sp.dma_start(cols[:, n:n + 1], v.rearrange("(p a) -> p a", a=1)).then_inc(S["w_in_a"], 16)
            for n, v in enumerate((Wg, Wv, Wd, Wo)):
                sp.dma_start(raw[:, R_GRU + n, :], v).then_inc(S["w_in_a"], 16)
            xr = x.rearrange("b s d -> s b d")
            sp.dma_start(x_all[:, 0:2, :], xr[:, 0:2, :]).then_inc(S["x_in"], 16)
            sp.dma_start(x_all[:, 2:TILES, :], xr[:, 2:TILES, :]).then_inc(S["x_in"], 16)
            sp.dma_start(raw[:, R_QKV:R_QKV + 3, :], Wqkv.rearrange("(n p) k -> p n k", p=P)).then_inc(S["w_in_b"], 16)
            sp.dma_start(raw[:, R_XWV, :], xWv).then_inc(S["w_in_b"], 16)
            sp.dma_start(raw[:, R_GATE:R_GATE + FF, :], Wgate.rearrange("(n p) k -> p n k", p=P)).then_inc(S["w_in_b"], 16)
            sp.dma_start(raw[:, R_UP:R_UP + FF, :], Wup.rearrange("(n p) k -> p n k", p=P)).then_inc(S["w_in_b"], 16)
            sp.dma_start(raw[:, R_OUT:R_OUT + FF, :], Wout.rearrange("p (n k) -> p n k", k=P)).then_inc(S["w_in_b"], 16)
            sp.dma_start(raw[:, R_WI:R_WI + EXPERTS, :], Wi.rearrange("e d h -> d e h")).then_inc(S["w_in_c"], 16)
            sp.dma_start(raw_xq[:], xWq).then_inc(S["w_in_c"], 16)
            sp.dma_start(raw_xk[:], xWk).then_inc(S["w_in_c"], 16)
            sp.dma_start(wmo_sb[:], Wmo.rearrange("e h d -> h e d")).then_inc(S["w_in_c"], 16)
            sp.dma_start(wr_sb[:], Wr).then_inc(S["w_in_c"], 16)
            sp.dma_start(mask_sb[:], mask).then_inc(S["w_in_c"], 16)
            sp.dma_start(xbv_sb[:], xbv.rearrange("(a n) -> a n", a=1).to_broadcast([P, P])).then_inc(S["w_in_c"], 16)

            def step(t, par):
                if (now := tile_at(t, par, FFN - 1)):
                    k, b = now
                    after(sp, "ctx_T_ps", k, alone=True)
                    sp.dma_start(ctx_sb[:, b, :], ctx[k]).then_inc(S["ctx_in"], 16)
                if (now := tile_at(t, par, MAX)):
                    k, b = now
                    after(sp, "max_mT", k + 1, alone=True)
                    sp.dma_start(q_stack[QROWS:SROWS, b, :, :], nmT[:, :]).then_inc(S["m_stacked"], 16)
                if (now := tile_at(t, par, QKV)):
                    k, b = now
                    after(sp, "qkv_hi", k + 1, alone=True)
                    after(sp, "qkv_mid", k + 1, alone=True)
                    after(sp, "qkv_lo", k + 1, alone=True)
                    qp = qk_parts[:, 0, :, :]
                    kp = qk_parts[:, 1, :, :]
                    sp.dma_start(scratch[b, 0:PARTS].rearrange("c r s -> r c s"), qp).then_inc(S["q_saved"], 16)
                    sp.dma_start(scratch[b, PARTS:QDUP].rearrange("c r s -> r c s"), qp[:, 0:QDUP - PARTS, :]).then_inc(S["q_saved"], 16)
                    sp.dma_start(scratch[b, QDUP:QDUP + PARTS].rearrange("c r s -> r c s"), kp).then_inc(S["q_saved"], 16)
                    after(sp, "q_saved", 48 * (k + 1), alone=True)
                    after(sp, "att_scores_ps", 4 * (k - 1), alone=True)
                    rot = scratch[b, 0:PARTS]
                    rot = bass.AP(rot.tensor, rot.offset, [[P * P, PARTS], [HEADS * P, PARTS * HD], [1, HEADS * P]])
                    sp.dma_start(q_stack[0:QROWS, b, :, :], rot).then_inc(S["q_stacked"], 16)
                    rep = scratch[b, QDUP:QDUP + PARTS]
                    rep = bass.AP(rep.tensor, rep.offset, [[0, PARTS], [HEADS * P, PARTS * HD], [1, HEADS * P]])
                    sp.dma_start(k_stack[0:QROWS, b, :, :], rep).then_inc(S["k_stacked"], 16)
                if (now := tile_at(t, par, MOE)):
                    k, b = now
                    after(sp, "moe_out", k + 1, alone=True)
                    sp.dma_start(out[k], out_sb[:, b, :]).then_inc(S["stored"], 16)

            sp.wait_ge(S["const_dve"], 5)
            steps(sp, step)
            sp.wait_ge(S["stored"], 16 * TILES)

        @block.gpsimd
        def _(pool):
            nc.gpsimd.memset(ident[:], 0.0).then_inc(S["const_pool"], 1)
            nc.gpsimd.memset(above[:], 0.0).then_inc(S["const_pool"], 1)
            nc.gpsimd.memset(below[:], 0.0).then_inc(S["const_pool"], 1)
            nc.gpsimd.memset(neghalf[:], -0.5).then_inc(S["const_pool"], 1)
            pool.wait_ge(S["const_pool"], 4)
            nc.gpsimd.affine_select(out=ident[:], in_=ident[:], compare_op=ALU.not_equal, fill=1.0, base=0,
                                    pattern=[[-1, P]], channel_multiplier=1).then_inc(S["const_pool"], 1)
            nc.gpsimd.affine_select(out=above[:], in_=above[:], compare_op=ALU.is_ge, fill=MASKED, base=0,
                                    pattern=[[0, 4], [-1, P]], channel_multiplier=1).then_inc(S["const_pool"], 1)
            nc.gpsimd.affine_select(out=below[:], in_=below[:], compare_op=ALU.is_ge, fill=MASKED, base=0,
                                    pattern=[[0, 4], [1, P]], channel_multiplier=-1).then_inc(S["const_pool"], 1)
            pool.wait_ge(S["const_pool"], 7)
            nc.gpsimd.tensor_copy(identb[:], ident[:]).then_inc(S["const_pool"], 1)

            def power(src, dst, ready, n, mean, rsd, scale, eps, tmp):
                after(pool, ready, n, alone=True)
                nc.gpsimd.tensor_scalar(tmp, src, scale, eps, ALU.mult, ALU.add).then_inc(S[mean], 1)
                after(pool, mean, n)
                nc.gpsimd.tensor_tensor(dst, tmp, neghalf[:], ALU.pow).then_inc(S[rsd], 1)

            def step(t, par):
                gru, qkv, mx, ffn = (tile_at(t, par, s) for s in (GRU, QKV, MAX, FFN))
                xat, moe = tile_at(t, par, XAT), tile_at(t, par, MOE)
                if gru:
                    power(ss[:, 0:1], rs[:, 0:1], "gru_ss", gru[0] + 1, "gru_ms", "gru_rs", 1.0 / P, RMS_EPS, ms[:, 0:1])
                if qkv:
                    power(ss[:, 1:2], rs[:, 1:2], "qkv_ss", qkv[0] + 1, "qkv_ms", "qkv_rs", 1.0 / P, RMS_EPS, ms[:, 1:2])
                if ffn:
                    power(ss[:, 2:3], rs[:, 2:3], "ffn_ss", ffn[0] + 1, "ffn_ms", "ffn_rs", 1.0 / P, RMS_EPS, ms[:, 2:3])
                if xat:
                    k, b = xat
                    after(pool, "ffn_y1", k + 1)
                    after(pool, "xat_z", k)
                    nc.gpsimd.tensor_tensor(y1b[:], y1[:, b, :], xbv_sb[:], ALU.add).then_inc(S["xat_y1b"], 1)
                if gru:
                    k, b = gru
                    after(pool, "gru_tanh", k + 1, alone=True)
                    after(pool, "gru_scan", k)
                    nc.gpsimd.tensor_scalar(gru_a[:], gru_t[:, 2, :], 0.499, 0.5, ALU.mult, ALU.add).then_inc(S["gru_decay"], 1)
                if ffn:
                    k, b = ffn
                    after(pool, "att_x2", k + 1)
                    after(pool, "ffn_z", k)
                    nc.gpsimd.tensor_tensor(x02[:], x_all[:, k, :], x2[:, b, :], ALU.add).then_inc(S["ffn_x02"], 1)
                if mx:
                    k, b = mx
                    after(pool, "max_max", 4 * (k + 1), alone=True)
                    after(pool, "max_mT_ps", k, alone=True)
                    nc.gpsimd.tensor_copy(nm_parts[:, 0, :], neg_max[:]).then_inc(S["max_n1"], 1)
                    after(pool, "max_n1", k + 1)
                    nc.gpsimd.tensor_tensor(nm_rest[:], neg_max[:], nm_parts[:, 0, :], ALU.subtract).then_inc(S["max_r1"], 1)
                    after(pool, "max_r1", k + 1, alone=True)
                    nc.gpsimd.tensor_copy(nm_parts[:, 1, :], nm_rest[:]).then_inc(S["max_n2"], 1)
                    after(pool, "max_n2", k + 1)
                    nc.gpsimd.tensor_tensor(nm_parts[:, 2, :], nm_rest[:], nm_parts[:, 1, :], ALU.subtract).then_inc(S["max_n3"], 1)
                if qkv:
                    k, b = qkv
                    after(pool, "qkv_mid", k + 1)
                    nc.gpsimd.tensor_tensor(qk_parts[:, :, 2, :], qk_rest[:], qk_parts[:, :, 1, :], ALU.subtract).then_inc(S["qkv_lo"], 1)
                if moe:
                    power(mv[:, 2, 1:2], lrs[:, 2:3], "moe_mv", moe[0] + 1, "moe_ve", "moe_rs", 1.0, LN_EPS, ve[:, 2:3])
                if xat:
                    power(mv[:, 1, 1:2], lrs[:, 1:2], "xat_mv", xat[0] + 1, "xat_ve", "xat_rs", 1.0, LN_EPS, ve[:, 1:2])
                if ffn:
                    power(mv[:, 0, 1:2], lrs[:, 0:1], "ffn_mv", ffn[0] + 1, "ffn_ve", "ffn_rs1", 1.0, LN_EPS, ve[:, 0:1])

            steps(pool, step)

        @block.tensor
        def _(pe):
            banks = [ps_scores[:], ps_probs[:], ps_wide[:, 0, :].rearrange("p (a b) -> p a b", a=4),
                     ps_wide[:, 1, :].rearrange("p (a b) -> p a b", a=4), ps_turn0[:], ps_turn1[:], ps_proj[:]]
            pe.wait_ge(S["const_pool"], 8)
            for g in range(NRAW // 4):
                if g == 0:
                    pe.wait_ge(S["w_in_a"], 160)
                if g == 1:
                    pe.wait_ge(S["w_in_b"], 80)
                if g == 5:
                    pe.wait_ge(S["w_in_c"], 112)
                for n in range(4):
                    last = nc.tensor.transpose(banks[g][:, n, :], raw[:, 4 * g + n, :], ident[:])
                last.then_inc(S["w_ps"], 1)
            nc.tensor.matmul(ps_y, raw_xk[:], raw_xq[:], start=True, stop=True).then_inc(S["w_ps"], 1)
            pe.wait_ge(S["w_act"], 4)
            pe.wait_ge(S["w_dve"], 8)
            for e in range(EXPERTS):
                last = nc.tensor.matmul(ps_wide[:, e // 4, (e % 4) * P:(e % 4) * P + P], wiT[:, e, :], wmo_sb[:, e, :], start=True, stop=True)
            last.then_inc(S["w_ps"], 1)
            pe.wait_ge(S["w_act"], 5)
            pe.wait_ge(S["const_dve"], 5)

            def step(t, par):
                gru, qkv, mx, att, ffn, xat, moe = (tile_at(t, par, s) for s in range(STAGES))

                def scores(n):
                    k, b = mx
                    if n == 0:
                        after(pe, "q_stacked", 16 * (k + 1))
                        after(pe, "k_stacked", 16 * (k + 1))
                    after(pe, "max_max", 4 * k + n)
                    for h in range(QUARTER):
                        nc.tensor.matmul(ps_scores[:, h, :], q_stack[0:QROWS, b, QUARTER * n + h, :],
                                                k_stack[0:QROWS, b, QUARTER * n + h, :], start=(h == 0), stop=False)
                    nc.tensor.matmul(ps_scores[:], identb[:], above[:], start=False, stop=True).then_inc(S["max_scores_ps"], 1)

                def scores_turned(n):
                    k, b = att
                    if n == 0:
                        after(pe, "m_stacked", 16 * (k + 1))
                    after(pe, "att_p", 4 * k + n)
                    for h in range(QUARTER):
                        nc.tensor.matmul(ps_probs[:, h, :], k_stack[0:SROWS, b, QUARTER * n + h, :],
                                                q_stack[0:SROWS, b, QUARTER * n + h, :], start=(h == 0), stop=False)
                    nc.tensor.matmul(ps_probs[:], identb[:], below[:], start=False, stop=True).then_inc(S["att_scores_ps"], 1)

                if mx:
                    scores(0)
                if xat:
                    k, b = xat
                    after(pe, "ffn_y1", k + 1)
                    region_free(pe, TURN0, t, 0)
                    nc.tensor.transpose(turn[0], y1[:, b, :], ident[:]).then_inc(S["xat_xT_ps"], 1)
                if moe:
                    k, b = moe
                    after(pe, "xat_y2", k + 1)
                    region_free(pe, TURN1, t, 0)
                    nc.tensor.transpose(turn[1], y2[:, b, :], ident[:]).then_inc(S["moe_xT_ps"], 1)
                if att:
                    scores_turned(0)
                if gru:
                    k, b = gru
                    after(pe, "gru_xn", k + 1)
                    region_free(pe, TURN0, t, 1)
                    nc.tensor.transpose(turn[0], xn[:, 0, :], ident[:]).then_inc(S["gru_xT_ps"], 1)
                if qkv:
                    k, b = qkv
                    after(pe, "qkv_xn", k + 1)
                    region_free(pe, TURN1, t, 1)
                    nc.tensor.transpose(turn[1], xn[:, 1, :], ident[:]).then_inc(S["qkv_xT_ps"], 1)
                if mx:
                    scores(1)
                if moe:
                    k, b = moe
                    after(pe, "moe_xT", k + 1)
                    region_free(pe, TURN1, t, 2)
                    nc.tensor.matmul(ps_logits, y2T[:], wr_sb[:], start=True, stop=True).then_inc(S["moe_logits_ps"], 1)
                    region_free(pe, WIDE, t, 0)
                    for j in range(2):
                        last = nc.tensor.matmul(ps_wide[:, j, :], y2T[:], w_moe[:, 4 * j:4 * j + 4, :], start=True, stop=True)
                    last.then_inc(S["moe_m_ps"], 1)
                if att:
                    scores_turned(1)
                if ffn:
                    k, b = ffn
                    after(pe, "ffn_xn", k + 1)
                    region_free(pe, TURN0, t, 2)
                    nc.tensor.transpose(turn[0], xn[:, 2, :], ident[:]).then_inc(S["ffn_xT_ps"], 1)
                if gru:
                    k, b = gru
                    after(pe, "gru_xT", k + 1)
                    region_free(pe, PROJ, t, 0)
                    for n in range(3):
                        last = nc.tensor.matmul(proj[:, n, :], gruT[:, n, :], xT[:, 0, :], start=True, stop=True)
                    last.then_inc(S["gru_gates_ps"], 1)
                if xat:
                    k, b = xat
                    after(pe, "xat_xT", k + 1)
                    after(pe, "ctx_kv", k + 1)
                    region_free(pe, SUM, t, 0)
                    nc.tensor.matmul(ps_y, y1T[:], ctx_kv[:, b, 0, :], start=True, stop=True).then_inc(S["xat_s_ps"], 1)
                if mx:
                    scores(2)
                    k, b = mx
                    after(pe, "qkv_xT", k + 1)
                    region_free(pe, PROJ, t, 1)
                    nc.tensor.matmul(proj[:, 0, :], qkv_xT[:, b, :], qkvT[:, 2, :], start=True, stop=True).then_inc(S["max_v_ps"], 1)
                if att:
                    scores_turned(2)
                if qkv:
                    k, b = qkv
                    after(pe, "qkv_xT", k + 1)
                    region_free(pe, PROJ, t, 2)
                    for n in range(2):
                        last = nc.tensor.matmul(proj[:, n, :], qkvT[:, n, :], qkv_xT[:, b, :], start=True, stop=True)
                    last.then_inc(S["qkv_ps"], 1)
                if mx:
                    scores(3)
                if gru:
                    k, b = gru
                    after(pe, "gru_scan", k + 1)
                    region_free(pe, TURN1, t, 3)
                    nc.tensor.transpose(turn[1], gru_h[:], ident[:]).then_inc(S["gru_hT_ps"], 1)
                if xat:
                    k, b = xat
                    after(pe, "xat_p", k + 1)
                    region_free(pe, TURN0, t, 3)
                    nc.tensor.transpose(turn[0], xat_p[:], ident[:]).then_inc(S["xat_pT_ps"], 1)
                if att:
                    scores_turned(3)
                if ffn:
                    k, b = ffn
                    after(pe, "ffn_xT", k + 1)
                    region_free(pe, WIDE, t, 1)
                    for g in range(2):
                        for n in range(FF):
                            last = nc.tensor.matmul(ps_wide[:, g, n * P:(n + 1) * P], guT[:, g, n * P:(n + 1) * P],
                                                    xT[:, 1, :], start=True, stop=True)
                    last.then_inc(S["ffn_gu_ps"], 1)
                if att:
                    k, b = att
                    after(pe, "max_v", k + 1)
                    region_free(pe, SUM, t, 1)
                    for h in range(HEADS):
                        if h % QUARTER == 0:
                            after(pe, "att_p", 4 * k + h // QUARTER + 1)
                        last = nc.tensor.matmul(ps_o[:, h, :], probs[:, h // QUARTER, h % QUARTER, :],
                                                values[:, b, h, :], start=True, stop=True)
                    last.then_inc(S["att_o_ps"], 1)
                if att:
                    k, b = att
                    after(pe, "att_o", k + 1)
                    region_free(pe, TURN1, t, 4)
                    nc.tensor.transpose(turn[1], att_o[:], ident[:]).then_inc(S["att_oT_ps"], 1)
                if mx:
                    k, b = mx
                    after(pe, "max_n3", k + 1, alone=True)
                    region_free(pe, TURN1, t, 5)
                    nc.tensor.transpose(ps_mT[0:PARTS * HEADS, :], nm_parts[:].rearrange("p c h -> p (c h)"),
                                        identb[:]).then_inc(S["max_mT_ps"], 1)
                if ffn:
                    k, b = ffn
                    after(pe, "ctx_in", 16 * (k + 1))
                    region_free(pe, TURN0, t, 4)
                    nc.tensor.transpose(turn[0], ctx_sb[:, b, :], ident[:]).then_inc(S["ctx_T_ps"], 1)
                if att:
                    k, b = att
                    after(pe, "att_oT", k + 1)
                    region_free(pe, SUM, t, 2)
                    nc.tensor.matmul(ps_y, att_oT[:], woT[:], start=True, stop=True).then_inc(S["att_y_ps"], 1)
                if ffn:
                    k, b = ffn
                    after(pe, "ctx_T", k + 1)
                    region_free(pe, PROJ, t, 3)
                    nc.tensor.matmul(proj[:, 0, :], w_kq[:], ctxT[:], start=True, stop=True)
                    nc.tensor.matmul(proj[:, 1, :], ctxT[:], xwvT[:], start=True, stop=True).then_inc(S["ctx_kv_ps"], 1)
                if xat:
                    k, b = xat
                    after(pe, "xat_pT", k + 1)
                    region_free(pe, SUM, t, 3)
                    nc.tensor.matmul(ps_y, xat_pT[:], ctx_kv[:, b, 1, :], start=True, stop=True).then_inc(S["xat_y_ps"], 1)
                if ffn:
                    k, b = ffn
                    after(pe, "ffn_h", k + 1)
                    region_free(pe, SUM, t, 4)
                    for n in range(FF):
                        last = nc.tensor.matmul(ps_y, hidden[:, n, :], outT[:, n, :], start=(n == 0), stop=(n == FF - 1))
                    last.then_inc(S["ffn_y_ps"], 1)

            steps(pe, step)

        @block.scalar
        def _(act):
            act.wait_ge(S["w_in_a"], 160)
            act.wait_ge(S["w_ps"], 3)
            nc.scalar.activation(guT[:, 0, :], ps_wide[:, 0, :], ACT.Copy, scale=cols[:, 2:3]).then_inc(S["w_act"], 1)
            act.wait_ge(S["w_ps"], 4)
            nc.scalar.activation(guT[:, 1, :], ps_wide[:, 1, :], ACT.Copy, scale=cols[:, 2:3]).then_inc(S["w_act"], 1)
            act.wait_ge(S["w_ps"], 5)
            nc.scalar.activation(outT[:], ps_turn0[:], ACT.Copy, scale=0.5).then_inc(S["w_act"], 1)
            act.wait_ge(S["w_ps"], 6)
            nc.scalar.copy(wiT[:, 0:4, :], ps_turn1[:]).then_inc(S["w_act"], 1)
            act.wait_ge(S["w_ps"], 9)
            nc.scalar.copy(w_moe[:].rearrange("p (g e) d -> p g (e d)", g=2), ps_wide[:]).then_inc(S["w_act"], 1)

            def step(t, par):
                gru, qkv, mx, att, ffn, xat, moe = (tile_at(t, par, s) for s in range(STAGES))

                def sum_of_squares(src, n, name):
                    nc.scalar.activation(junk[:, n, :], src, ACT.Square, accum_out=ss[:, n:n + 1]).then_inc(S[name], 1)

                def gru_gates():
                    k, b = gru
                    after(act, "gru_gates_ps", k + 1)
                    after(act, "gru_xs", k)
                    after(act, "gru_decay", k)
                    nc.scalar.activation(gru_t[:, 0, :], proj[:, 0, :], ACT.Tanh, bias=half_b[:, 0:1], scale=0.5)
                    nc.scalar.activation(gru_t[:, 1, :], proj[:, 1, :], ACT.Tanh, bias=cols[:, 4:5])
                    nc.scalar.activation(gru_t[:, 2, :], proj[:, 2, :], ACT.Tanh, bias=half_b[:, 1:2], scale=0.5).then_inc(S["gru_tanh"], 1)

                def exponentials(n):
                    k, b = att
                    after(act, "att_scores_ps", 4 * k + n + 1)
                    after(act, "att_o_ps", k)
                    nc.scalar.activation(probs[:, n, :, :], ps_probs[:], ACT.Exp, scale=HD ** -0.5).then_inc(S["att_p"], 1)

                if qkv:
                    k, b = qkv
                    after(act, "gru_x1", k + 1)
                    after(act, "qkv_ms", k)
                    sum_of_squares(x1_all[:, k, :], 1, "qkv_ss")
                if ffn:
                    k, b = ffn
                    after(act, "att_x2", k + 1)
                    after(act, "ffn_ms", k)
                    sum_of_squares(x2[:, b, :], 2, "ffn_ss")
                if xat:
                    k, b = xat
                    after(act, "xat_xT_ps", k + 1)
                    after(act, "xat_s_ps", k)
                    nc.scalar.copy(y1T[:], turn[0]).then_inc(S["xat_xT"], 1)
                if moe:
                    k, b = moe
                    after(act, "moe_xT_ps", k + 1)
                    after(act, "moe_m_ps", k)
                    nc.scalar.copy(y2T[:], turn[1]).then_inc(S["moe_xT"], 1)
                if gru:
                    k, b = gru
                    after(act, "gru_xT_ps", k + 1)
                    after(act, "gru_gates_ps", k)
                    nc.scalar.copy(xT[:, 0, :], turn[0]).then_inc(S["gru_xT"], 1)
                if att:
                    exponentials(0)
                if qkv:
                    k, b = qkv
                    after(act, "qkv_xT_ps", k + 1)
                    after(act, "max_v_ps", k - 1)
                    nc.scalar.copy(qkv_xT[:, b, :], turn[1]).then_inc(S["qkv_xT"], 1)
                if ffn:
                    k, b = ffn
                    after(act, "ffn_xT_ps", k + 1)
                    after(act, "ffn_gu_ps", k)
                    nc.scalar.copy(xT[:, 1, :], turn[0]).then_inc(S["ffn_xT"], 1)
                if att:
                    exponentials(1)
                if moe:
                    k, b = moe
                    after(act, "moe_logits_ps", k + 1)
                    after(act, "moe_c", k)
                    nc.scalar.copy(moe_lg[:], ps_logits).then_inc(S["moe_lg"], 1)
                if gru:
                    gru_gates()
                if moe:
                    k, b = moe
                    after(act, "moe_negm", k + 1)
                    after(act, "moe_c", k)
                    nc.scalar.activation(moe_e[:], moe_lg[:], ACT.Exp, bias=moe_m[:, 0:1],
                                         accum_out=moe_l[:, 0:1]).then_inc(S["moe_e"], 1)
                if xat:
                    k, b = xat
                    after(act, "xat_negm", k + 1)
                    after(act, "xat_pT_ps", k)
                    after(act, "xat_rd", k)
                    nc.scalar.activation(xat_p[:], xat_s[:], ACT.Exp, bias=xat_m[:, 1:2],
                                         accum_out=xat_l[:, 0:1]).then_inc(S["xat_p"], 1)
                if mx:
                    k, b = mx
                    after(act, "max_v_ps", k + 1)
                    after(act, "att_o_ps", k - 1)
                    nc.scalar.copy(values[:, b, :, 0:HD], proj[:, 0, :].rearrange("p (h d) -> p h d", h=HEADS)).then_inc(S["max_v"], 1)
                if att:
                    exponentials(2)
                if qkv:
                    k, b = qkv
                    after(act, "qkv_ps", k + 1)
                    after(act, "q_saved", 48 * k)
                    nc.scalar.copy(qk_parts[:, :, 0, :], proj[:, 0:2, :]).then_inc(S["qkv_hi"], 1)
                if xat:
                    k, b = xat
                    after(act, "xat_pT_ps", k + 1)
                    after(act, "xat_y_ps", k)
                    nc.scalar.copy(xat_pT[:], turn[0]).then_inc(S["xat_pT"], 1)
                if att:
                    exponentials(3)
                if qkv:
                    k, b = qkv
                    after(act, "qkv_rest", k + 1)
                    nc.scalar.copy(qk_parts[:, :, 1, :], qk_rest[:]).then_inc(S["qkv_mid"], 1)
                if ffn:
                    k, b = ffn
                    after(act, "ffn_gu_ps", k + 1)
                    after(act, "ffn_t1", k)
                    nc.scalar.activation(gate_t[:], ps_wide[:, 0, :], ACT.Tanh, scale=0.5).then_inc(S["ffn_tanh"], 1)
                if att:
                    k, b = att
                    after(act, "att_oT_ps", k + 1)
                    after(act, "att_y_ps", k)
                    nc.scalar.copy(att_oT[:], turn[1]).then_inc(S["att_oT"], 1)
                if mx:
                    k, b = mx
                    after(act, "max_mT_ps", k + 1)
                    after(act, "m_stacked", 16 * k)
                    nc.scalar.copy(nmT[:], ps_mT[0:PARTS * HEADS, :]).then_inc(S["max_mT"], 1)
                if ffn:
                    k, b = ffn
                    after(act, "ctx_T_ps", k + 1)
                    after(act, "ctx_kv_ps", k)
                    nc.scalar.copy(ctxT[:], turn[0]).then_inc(S["ctx_T"], 1)
                    after(act, "ctx_kv_ps", k + 1)
                    after(act, "xat_y_ps", k - 1)
                    nc.scalar.copy(ctx_kv[:, b, :, :], proj[:, 0:2, :]).then_inc(S["ctx_kv"], 1)
                gru_square(t + 1)

            def gru_square(k):
                if isinstance(k, int) and k >= TILES:
                    return
                after(act, "gru_ms", k)
                sum_of_squares_gru(k)

            def sum_of_squares_gru(k):
                nc.scalar.activation(junk[:, 0, :], x_all[:, k, :], ACT.Square, accum_out=ss[:, 0:1]).then_inc(S["gru_ss"], 1)

            act.wait_ge(S["x_in"], 32)
            gru_square(0)
            for t in range(LOOP):
                step(t, t % 2)
            with act.Fori(LOOP, TILES - 3, 2) as i:
                step(i, 0)
                step(i + 1, 1)
            for t in range(TILES - 2, LAST):
                step(t, t % 2)

        @block.vector
        def _(dve):
            nc.vector.memset(q_stack[:], 1.0).then_inc(S["const_dve"], 1)
            nc.vector.memset(k_stack[:], 1.0).then_inc(S["const_dve"], 1)
            nc.vector.memset(values[:], 1.0).then_inc(S["const_dve"], 1)
            nc.vector.memset(ones8[:], 1.0).then_inc(S["const_dve"], 1)
            dve.wait_ge(S["w_in_a"], 160)
            dve.wait_ge(S["w_ps"], 1)
            nc.vector.tensor_scalar(gruT[:], ps_scores[:, 0:3, :], cols[:, 0:1], None, ALU.mult).then_inc(S["w_dve"], 1)
            nc.vector.tensor_copy(woT[:], ps_scores[:, 3, :]).then_inc(S["w_dve"], 1)
            nc.vector.tensor_scalar(half_b[:, 0:1], cols[:, 3:4], 0.5, None, ALU.mult)
            nc.vector.tensor_scalar(half_b[:, 1:2], cols[:, 5:6], 0.5, None, ALU.mult).then_inc(S["const_dve"], 1)
            dve.wait_ge(S["w_ps"], 2)
            for n in range(2):
                nc.vector.tensor_scalar(qkvT[:, n, :].rearrange("p (d h) -> p h d", d=HD),
                                        ps_probs[:, n, :].rearrange("p (h d) -> p h d", d=HD),
                                        cols[:, 1:2], None, ALU.mult).then_inc(S["w_dve"], 1)
            nc.vector.tensor_scalar(qkvT[:, 2, :], ps_probs[:, 2, :], cols[:, 1:2], None, ALU.mult).then_inc(S["w_dve"], 1)
            nc.vector.tensor_copy(xwvT[:], ps_probs[:, 3, :]).then_inc(S["w_dve"], 1)
            dve.wait_ge(S["w_ps"], 7)
            nc.vector.tensor_copy(wiT[:, 4:8, :], ps_proj[:]).then_inc(S["w_dve"], 1)
            dve.wait_ge(S["w_ps"], 8)
            nc.vector.tensor_scalar(w_kq[:], ps_y, P ** -0.5, None, ALU.mult).then_inc(S["w_dve"], 1)

            def normalize(n, k, src, dst, rsd, done):
                after(dve, rsd, k + 1)
                nc.vector.tensor_scalar(dst, src, rs[:, n:n + 1], None, ALU.mult).then_inc(S[done], 1)

            def layernorm_stats(n, k, src, ready, stat, agg):
                after(dve, ready, k + 1)
                nc.vector.bn_stats(stats[:, n, :], src).then_inc(S[stat], 1)
                after(dve, stat, k + 1, alone=True)
                nc.vector.bn_aggr(mv[:, n, :], stats[:, n, :]).then_inc(S[agg], 1)

            def layernorm_apply(n, k, src, dst, rsd, done):
                after(dve, rsd, k + 1)
                nc.vector.tensor_scalar(dst, src, mv[:, n, 0:1], lrs[:, n:n + 1], ALU.subtract, ALU.mult).then_inc(S[done], 1)

            def step(t, par):
                gru, qkv, mx, att, ffn, xat, moe = (tile_at(t, par, s) for s in range(STAGES))

                def maxima(n):
                    k, b = mx
                    after(dve, "max_scores_ps", 4 * k + n + 1)
                    if n == 0:
                        after(dve, "max_n3", k)
                    nc.vector.tensor_reduce(neg_max[:, QUARTER * n:QUARTER * n + QUARTER], ps_scores[:], AX_X,
                                            ALU.max, negate=True).then_inc(S["max_max"], 1)

                if gru:
                    k, b = gru
                    after(dve, "gru_xT_ps", k)
                    normalize(0, k, x_all[:, k, :], xn[:, 0, :], "gru_rs", "gru_xn")
                if mx:
                    maxima(0)
                if qkv:
                    k, b = qkv
                    after(dve, "qkv_xT_ps", k)
                    normalize(1, k, x1_all[:, k, :], xn[:, 1, :], "qkv_rs", "qkv_xn")
                if mx:
                    maxima(1)
                if ffn:
                    k, b = ffn
                    after(dve, "ffn_xT_ps", k)
                    normalize(2, k, x2[:, b, :], xn[:, 2, :], "ffn_rs", "ffn_xn")
                if moe:
                    k, b = moe
                    after(dve, "moe_lg", k + 1, alone=True)
                    nc.vector.max(top[:], moe_lg[:]).then_inc(S["moe_top"], 1)
                    after(dve, "moe_top", k + 1)
                    nc.vector.tensor_scalar(moe_m[:, 0:1], top[:, 0:1], -1.0, None, ALU.mult).then_inc(S["moe_negm"], 1)
                    nc.vector.tensor_scalar(moe_eq[:], moe_lg[:], top[:, 1:2], None, ALU.is_equal).then_inc(S["moe_eq"], 1)
                    nc.vector.tensor_scalar(moe_gt[:], moe_lg[:], top[:, 1:2], None, ALU.is_gt, ALU.add,
                                            accum_out=moe_n[:]).then_inc(S["moe_gt"], 1)
                    after(dve, "moe_eq", k + 1)
                    nc.vector.tensor_tensor_scan(moe_cum[:], ones8[:], moe_eq[:], 0.0, ALU.mult, ALU.add).then_inc(S["moe_cum"], 1)
                    after(dve, "moe_cum", k + 1)
                    after(dve, "moe_gt", k + 1)
                    nc.vector.tensor_scalar(moe_lt[:], moe_cum[:], moe_n[:], 2.5, ALU.add, ALU.is_lt).then_inc(S["moe_lt"], 1)
                if xat:
                    k, b = xat
                    after(dve, "xat_s_ps", k + 1, alone=True)
                    nc.vector.tensor_tensor_reduce(xat_s[:], ps_y, mask_sb[:], 1.0, -3.4e38, ALU.add, ALU.max,
                                                   xat_m[:, 0:1]).then_inc(S["xat_sm"], 1)
                if moe:
                    k, b = moe
                    after(dve, "moe_lt", k + 1)
                    nc.vector.tensor_tensor(moe_both[:], moe_lt[:], moe_eq[:], ALU.mult).then_inc(S["moe_both"], 1)
                if xat:
                    k, b = xat
                    after(dve, "xat_sm", k + 1)
                    nc.vector.tensor_scalar(xat_m[:, 1:2], xat_m[:, 0:1], -1.0, None, ALU.mult).then_inc(S["xat_negm"], 1)
                if moe:
                    k, b = moe
                    after(dve, "moe_both", k + 1)
                    nc.vector.tensor_tensor(moe_sel[:], moe_both[:], moe_gt[:], ALU.add).then_inc(S["moe_sel"], 1)
                    after(dve, "moe_e", k + 1)
                    nc.vector.reciprocal(moe_l[:, 1:2], moe_l[:, 0:1]).then_inc(S["moe_rd"], 1)
                    after(dve, "moe_sel", k + 1)
                    after(dve, "moe_rd", k + 1)
                    nc.vector.scalar_tensor_tensor(moe_c[:], moe_sel[:], moe_l[:, 1:2], moe_e[:], ALU.mult, ALU.mult).then_inc(S["moe_c"], 1)
                if mx:
                    maxima(2)
                if gru:
                    k, b = gru
                    after(dve, "gru_tanh", k + 1)
                    nc.vector.scalar_tensor_tensor(gru_xs[:], gru_t[:, 0, :], 1.0, gru_t[:, 1, :], ALU.add, ALU.mult).then_inc(S["gru_xs"], 1)
                if moe:
                    k, b = moe
                    after(dve, "moe_m_ps", k + 1)
                    after(dve, "moe_c", k + 1)
                    for e in range(EXPERTS):
                        if e:
                            after(dve, "moe_acc", (EXPERTS - 1) * k + e)
                        nc.vector.scalar_tensor_tensor(acc[:, e % 2, :] if e < EXPERTS - 1 else z[:, 2, :],
                                                       ps_wide[:, e // 4, (e % 4) * P:(e % 4) * P + P], moe_c[:, e:e + 1],
                                                       acc[:, (e + 1) % 2, :] if e else y2[:, b, :],
                                                       ALU.mult, ALU.add).then_inc(S["moe_acc" if e < EXPERTS - 1 else "moe_z"], 1)
                if gru:
                    k, b = gru
                    after(dve, "gru_xs", k + 1)
                    after(dve, "gru_decay", k + 1)
                    after(dve, "gru_hT_ps", k)
                    nc.vector.tensor_tensor_scan(gru_h[:], gru_a[:], gru_xs[:], 0.0, ALU.mult, ALU.add).then_inc(S["gru_scan"], 1)
                if mx:
                    maxima(3)
                if qkv:
                    k, b = qkv
                    after(dve, "qkv_hi", k + 1)
                    after(dve, "qkv_lo", k)
                    nc.vector.tensor_tensor(qk_rest[:], proj[:, 0:2, :], qk_parts[:, :, 0, :], ALU.subtract).then_inc(S["qkv_rest"], 1)
                if moe:
                    k, b = moe
                    layernorm_stats(2, k, z[:, 2, :], "moe_z", "moe_stats", "moe_mv")
                if gru:
                    k, b = gru
                    after(dve, "gru_hT_ps", k + 1)
                    nc.vector.scalar_tensor_tensor(x1_all[:, k, :], turn[1], 0.5, x_all[:, k, :], ALU.mult, ALU.add).then_inc(S["gru_x1"], 1)
                if att:
                    k, b = att
                    after(dve, "att_o_ps", k + 1)
                    nc.vector.reciprocal(att_rd[:], ps_o[:, :, HD]).then_inc(S["att_rd"], 1)
                    after(dve, "att_rd", k + 1)
                    after(dve, "att_oT_ps", k)
                    nc.vector.tensor_tensor(att_o[:].rearrange("p (h d) -> p h d", h=HEADS), ps_o[:, :, 0:HD],
                                            att_rd[:].unsqueeze(2).to_broadcast([P, HEADS, HD]), ALU.mult).then_inc(S["att_o"], 1)
                if moe:
                    k, b = moe
                    after(dve, "stored", 16 * k)
                    layernorm_apply(2, k, z[:, 2, :], out_sb[:, b, :], "moe_rs", "moe_out")
                if ffn:
                    k, b = ffn
                    after(dve, "ffn_tanh", k + 1)
                    nc.vector.scalar_tensor_tensor(gate_1[:], gate_t[:], 1.0, ps_wide[:, 0, :], ALU.add, ALU.mult).then_inc(S["ffn_t1"], 1)
                    after(dve, "ffn_t1", k + 1)
                    after(dve, "ffn_y_ps", k)
                    nc.vector.tensor_tensor(hidden[:].rearrange("p a b -> p (a b)"), gate_1[:], ps_wide[:, 1, :], ALU.mult).then_inc(S["ffn_h"], 1)
                if att:
                    k, b = att
                    after(dve, "att_y_ps", k + 1)
                    nc.vector.tensor_tensor(x2[:, b, :], ps_y, x1_all[:, k, :], ALU.add).then_inc(S["att_x2"], 1)
                if xat:
                    k, b = xat
                    after(dve, "xat_p", k + 1)
                    nc.vector.reciprocal(xat_l[:, 1:2], xat_l[:, 0:1]).then_inc(S["xat_rd"], 1)
                    after(dve, "xat_rd", k + 1)
                    after(dve, "xat_y_ps", k + 1)
                    after(dve, "xat_y1b", k + 1)
                    nc.vector.scalar_tensor_tensor(z[:, 1, :], ps_y, xat_l[:, 1:2], y1b[:], ALU.mult, ALU.add).then_inc(S["xat_z"], 1)
                    layernorm_stats(1, k, z[:, 1, :], "xat_z", "xat_stats", "xat_mv")
                if ffn:
                    k, b = ffn
                    after(dve, "ffn_y_ps", k + 1)
                    after(dve, "ffn_x02", k + 1)
                    nc.vector.tensor_tensor(z[:, 0, :], ps_y, x02[:], ALU.add).then_inc(S["ffn_z"], 1)
                if xat:
                    k, b = xat
                    layernorm_apply(1, k, z[:, 1, :], y2[:, b, :], "xat_rs", "xat_y2")
                if ffn:
                    k, b = ffn
                    layernorm_stats(0, k, z[:, 0, :], "ffn_z", "ffn_stats", "ffn_mv")
                    layernorm_apply(0, k, z[:, 0, :], y1[:, b, :], "ffn_rs1", "ffn_y1")

            dve.wait_ge(S["x_in"], 32)
            dve.wait_ge(S["w_in_c"], 112)
            steps(dve, step)


_INS = ['x', 'ctx_1024', 'mask_SxS2_fk0', 'L0_attn_w_rms_mix', 'L0_attn_Wg', 'L0_attn_bg', 'L0_attn_Wv',
        'L0_attn_bv', 'L0_attn_Wd', 'L0_attn_bd', 'L0_attn_w_rms_attn', 'L0_attn_Wqkv', 'L0_attn_Wo',
        'L0_attn_w_rms_ffn', 'L0_attn_Wgate', 'L0_attn_Wup', 'L0_attn_Wout', 'L0_xattn_Wq', 'L0_xattn_Wk',
        'L0_xattn_Wv', 'L0_xattn_bv', 'L0_ffn_Wr', 'L0_ffn_Wi', 'L0_ffn_Wo']


def kernel(**inputs):
    import numpy as _np
    import concourse.bacc as _bacc
    from concourse import mybir as _mybir
    from concourse.bass_utils import run_bass_kernel_spmd as _run

    nc = _bacc.Bacc("TRN2", target_bir_lowering=False, num_devices=1)
    arrays, args = {}, []
    for name in _INS:
        a = _np.ascontiguousarray(inputs[name])
        arrays[f"in_{name}_dram"] = a
        args.append(nc.dram_tensor(f"in_{name}_dram", a.shape, _mybir.dt.from_np(a.dtype), kind="ExternalInput").ap())
    shape = inputs["x"].shape
    args.append(nc.dram_tensor("out_0_dram", shape, _mybir.dt.float32, kind="ExternalOutput").ap())
    decoder_layer(nc, *args)
    r = _run(nc, [arrays], core_ids=[0])
    return r.results[0]["out_0_dram"]
```

```python
from contextlib import ExitStack

import concourse.bass as bass
from concourse import mybir

P = 128
HEADS = 16
HD = P // HEADS
EXPERTS = 8
FF = 4
PARTS = 3
PAIRS = PARTS * PARTS
QROWS = PAIRS * HD
SROWS = QROWS + PARTS
QUARTER = HEADS // 4
RMS_EPS = 1e-6
LN_EPS = 1e-5
MASKED = -1e30

MAX_LAG = 8

USERS = [
    [("att_values", 5, "att_o"),
     ("gru_gates", 1, "gru_tanh"),
     ("xat_turn_probs", 7, "xat_pT"),
     ("v_project", 3, "max_v")],
    [("qkv_turn", 2, "qkv_xT"),
     ("qk_project", 2, "qkv_rest"),
     ("moe_turn", 8, "moe_xT"),
     ("moe_logits", 8, "moe_lg"),
     ("ffn_down", 6, "ffn_z"),
     ("gru_turn_back", 1, "gru_x1"),
     ("ffn_turn", 5, "ffn_xT")],
    [("ctx_turn", 5, "ctx_T"),
     ("xat_turn", 7, "xat_xT"),
     ("xat_scores", 7, "xat_sm"),
     ("max_turn", 4, "max_mT"),
     ("xat_values", 7, "xat_z")],
    [("att_turn", 5, "att_oT"),
     ("att_project", 5, "att_x2"),
     ("ctx_project", 5, "ctx_kv"),
     ("gru_turn", 0, "gru_xT")],
    [("moe_experts_0", 8, "moe_low"),
     ("ffn_gate", 5, "ffn_t1")],
    [("ffn_up", 6, "ffn_h"),
     ("moe_experts_1", 8, "moe_z")],
]
BANK = {piece: n for n, users in enumerate(USERS) for piece, _, _ in users}

ALU = mybir.AluOpType
ACT = mybir.ActivationFunctionType
F32 = mybir.dt.float32
BF16 = mybir.dt.bfloat16
AX_X = mybir.AxisListType.X

TILE_SEMS = """
gru_ss gru_ms gru_rs gru_xn gru_xT_ps gru_xT gru_gates_ps gru_tanh gru_xs gru_decay gru_scan gru_hT_ps gru_x1
qkv_ss qkv_ms qkv_rs qkv_xn qkv_xT_ps qkv_xT qkv_ps qkv_hi qkv_rest qkv_mid qkv_lo
max_scores_ps max_max max_n1 max_r1 max_n2 max_n3 max_mT_ps max_mT max_v_ps max_v
att_scores_ps att_p att_o_ps att_rd att_o att_oT_ps att_oT att_y_ps att_x2
ffn_ss ffn_ms ffn_rs ffn_xn ffn_xT_ps ffn_xT ffn_gate_ps ffn_up_ps ffn_tanh ffn_t1 ffn_h ffn_x02 ffn_y_ps ffn_z
ffn_stats ffn_mv ffn_ve ffn_rs1 ffn_y1 ctx_T_ps ctx_T ctx_kv_ps ctx_kv
xat_xT_ps xat_xT xat_s_ps xat_sm xat_negm xat_p xat_pT_ps xat_pT xat_rd xat_y1b xat_y_ps xat_z
xat_stats xat_mv xat_ve xat_rs xat_y2
moe_xT_ps moe_xT moe_logits_ps moe_top moe_negm moe_e moe_gt moe_eq moe_cum moe_lt moe_both moe_sel moe_rd moe_c moe_lg
moe_m0_ps moe_m1_ps moe_acc moe_low moe_z moe_stats moe_mv moe_ve moe_rs moe_out
""".split()
DMA_SEMS = "x_in ctx_in w_in_a w_in_b w_in_c parts_saved q_stacked k_stacked m_stacked stored".split()
SETUP_SEMS = "const_pool const_dve w_ps w_dve w_act".split()


def decoder_layer(nc, x, ctx, mask, w_mix, Wg, bg, Wv, bv, Wd, bd, w_attn, Wqkv, Wo, w_ffn, Wgate, Wup,
                  Wout, xWq, xWk, xWv, xbv, Wr, Wi, Wmo, out):
    TILES = x.shape[0]
    LAST = TILES + MAX_LAG
    LOOP = MAX_LAG + 1 + (MAX_LAG + 1) % 2
    assert TILES % 2 == 0 and TILES > LOOP and x.shape[1:] == (P, P)

    with ExitStack() as stack:
        def sb(name, shape, dt=F32):
            return stack.enter_context(nc.sbuf_tensor(name, shape, dt))

        def psum(name, shape, dt=F32):
            return stack.enter_context(nc.psum_tensor(name, shape, dt))

        S = {name: stack.enter_context(nc.semaphore(name)) for name in TILE_SEMS + DMA_SEMS + SETUP_SEMS}

        ps_scores = psum("ps_scores", [P, QUARTER, P])
        ps_probs = psum("ps_probs", [P, QUARTER, P])
        banks = [psum(f"ps_{n}", [P, 4, P]) for n in range(6)]

        def view(fill):
            return banks[BANK[fill]][:]

        def as_one(ap):
            return ap.rearrange("p a b -> p (a b)")

        def o_view():
            return as_one(view("att_values"))[:, 0:HEADS * (HD + 1)].rearrange("p (h e) -> p h e", h=HEADS)

        ident = sb("ident", [P, P])
        identb = sb("identb", [P, P], BF16)
        above = sb("above", [P, 4, P], BF16)
        below = sb("below", [P, 4, P], BF16)
        neghalf = sb("neghalf", [P, 1])
        ones8 = sb("ones8", [P, EXPERTS])
        mask_sb = sb("mask_sb", [P, P])
        xbv_sb = sb("xbv_sb", [P, P])
        cols = sb("cols", [P, 6])
        half_b = sb("half_b", [P, 2])
        NRAW = 28
        raw = sb("raw", [P, NRAW, P])
        R_GRU, R_WO, R_QKV, R_XWV, R_GATE, R_UP, R_OUT, R_WI = 0, 3, 4, 7, 8, 12, 16, 20
        raw_xq = sb("raw_xq", [P, P])
        raw_xk = sb("raw_xk", [P, P])
        wr_sb = sb("wr_sb", [P, EXPERTS])
        wmo_sb = sb("wmo_sb", [P, EXPERTS, P])
        gruT = sb("gruT", [P, 3, P])
        woT = sb("woT", [P, P])
        qkvT = sb("qkvT", [P, 3, P])
        xwvT = sb("xwvT", [P, P])
        guT = sb("guT", [P, 2, FF * P])
        outT = sb("outT", [P, FF, P])
        wiT = sb("wiT", [P, EXPERTS, P])
        w_kq = sb("w_kq", [P, P])
        w_moe = sb("w_moe", [P, EXPERTS, P])

        x_all = sb("x_all", [P, TILES, P])
        x1_all = sb("x1_all", [P, TILES, P])
        junk = sb("junk", [P, 3, P])
        ss = sb("ss", [P, 3])
        ms = sb("ms", [P, 3])
        rs = sb("rs", [P, 3])
        xn = sb("xn", [P, 3, P])
        xT = sb("xT", [P, 2, P])
        qkv_xT = sb("qkv_xT", [P, 2, P])
        gru_t = sb("gru_t", [P, 3, P])
        gru_xs = sb("gru_xs", [P, P])
        gru_a = sb("gru_a", [P, P])
        gru_h = sb("gru_h", [P, P])
        qk_rest = sb("qk_rest", [P, 2, P])
        qk_parts = sb("qk_parts", [P, 2, 2, PARTS, P], BF16)
        q_stack = sb("q_stack", [P, 2, HEADS, P], BF16)
        k_stack = sb("k_stack", [P, 2, HEADS, P], BF16)
        neg_max = sb("neg_max", [P, HEADS])
        nm_rest = sb("nm_rest", [P, HEADS])
        nm_parts = sb("nm_parts", [P, PARTS, HEADS], BF16)
        nmT = sb("nmT", [PARTS * HEADS, P], BF16)
        values = sb("values", [P, 2, HEADS, HD + 1])
        probs = sb("probs", [P, 4, QUARTER, P])
        att_rd = sb("att_rd", [P, HEADS])
        att_o = sb("att_o", [P, P])
        att_oT = sb("att_oT", [P, P])
        x2 = sb("x2", [P, 2, P])
        x02 = sb("x02", [P, P])
        gate_t = sb("gate_t", [P, FF * P])
        gate_1 = sb("gate_1", [P, FF * P])
        hidden = sb("hidden", [P, FF, P])
        z = sb("z", [P, 3, P])
        stats = sb("stats", [P, 3, 6])
        mv = sb("mv", [P, 3, 2])
        ve = sb("ve", [P, 3])
        lrs = sb("lrs", [P, 3])
        y1 = sb("y1", [P, 2, P])
        ctx_sb = sb("ctx_sb", [P, 2, P])
        ctxT = sb("ctxT", [P, P])
        ctx_kv = sb("ctx_kv", [P, 2, 2, P])
        y1T = sb("y1T", [P, P])
        xat_s = sb("xat_s", [P, P])
        xat_m = sb("xat_m", [P, 2])
        xat_p = sb("xat_p", [P, P])
        xat_l = sb("xat_l", [P, 2])
        xat_pT = sb("xat_pT", [P, P])
        y1b = sb("y1b", [P, P])
        y2 = sb("y2", [P, 2, P])
        y2T = sb("y2T", [P, P])
        top = sb("top", [P, EXPERTS])
        moe_lg = sb("moe_lg", [P, EXPERTS])
        moe_m = sb("moe_m", [P, 2])
        moe_e = sb("moe_e", [P, EXPERTS])
        moe_l = sb("moe_l", [P, 2])
        moe_gt = sb("moe_gt", [P, EXPERTS])
        moe_n = sb("moe_n", [P, 1])
        moe_eq = sb("moe_eq", [P, EXPERTS])
        moe_cum = sb("moe_cum", [P, EXPERTS])
        moe_lt = sb("moe_lt", [P, EXPERTS])
        moe_both = sb("moe_both", [P, EXPERTS])
        moe_sel = sb("moe_sel", [P, EXPERTS])
        moe_c = sb("moe_c", [P, EXPERTS])
        acc = sb("acc", [P, 2, P])
        out_sb = sb("out_sb", [P, 2, P])
        scratch = nc.dram_tensor("qk_scratch", [2, 3 * PARTS - 1, P, P], BF16).ap()

        def after(eng, name, n):
            if isinstance(n, int) and n <= 0:
                return
            eng.wait_ge(S[name], n)

        def after_all(eng, *waits):
            waits = [(name, n) for name, n in waits if not isinstance(n, int) or n > 0]
            if any(not isinstance(n, int) for _, n in waits):
                for _, n in waits:
                    if not isinstance(n, int):
                        eng.lower_val(n)
                eng.wait_ge(S["const_pool"], 8)
            for name, n in waits:
                eng.wait_ge(S[name], n)

        def run(t, par, lag, piece, *more):
            k = t - lag
            if isinstance(t, int) and not 0 <= k < TILES:
                return
            piece(k, (par + lag) % 2, *more)

        def steps(eng, step):
            for t in range(LOOP):
                step(t, t % 2)
            with eng.Fori(LOOP, TILES - 1, 2) as i:
                step(i, 0)
                step(i + 1, 1)
            for t in range(TILES, LAST):
                step(t, t % 2)

        def last_use(k, fill):
            users = USERS[BANK[fill]]
            me = [u[0] for u in users].index(fill)
            for back in range(1, len(users) + 1):
                n = me - back
                _, lag, name = users[n]
                other = k + users[me][1] - lag - (1 if n < 0 else 0)
                if not isinstance(other, int) or 0 <= other < TILES:
                    return name, other + 1
            return users[me][2], 0

        def bank_free(eng, k, fill):
            after(eng, *last_use(k, fill))

        block = stack.enter_context(nc.Block())

        @block.sync
        def _(sp):
            for n, v in enumerate((w_mix, w_attn, w_ffn, bg, bv, bd)):
                sp.dma_start(cols[:, n:n + 1], v.rearrange("(p a) -> p a", a=1)).then_inc(S["w_in_a"], 16)
            for n, v in enumerate((Wg, Wv, Wd, Wo)):
                sp.dma_start(raw[:, R_GRU + n, :], v).then_inc(S["w_in_a"], 16)
            xr = x.rearrange("b s d -> s b d")
            sp.dma_start(x_all[:, 0:2, :], xr[:, 0:2, :]).then_inc(S["x_in"], 16)
            sp.dma_start(x_all[:, 2:TILES, :], xr[:, 2:TILES, :]).then_inc(S["x_in"], 16)
            sp.dma_start(raw[:, R_QKV:R_QKV + 3, :], Wqkv.rearrange("(n p) k -> p n k", p=P)).then_inc(S["w_in_b"], 16)
            sp.dma_start(raw[:, R_XWV, :], xWv).then_inc(S["w_in_b"], 16)
            sp.dma_start(raw[:, R_GATE:R_GATE + FF, :], Wgate.rearrange("(n p) k -> p n k", p=P)).then_inc(S["w_in_b"], 16)
            sp.dma_start(raw[:, R_UP:R_UP + FF, :], Wup.rearrange("(n p) k -> p n k", p=P)).then_inc(S["w_in_b"], 16)
            sp.dma_start(raw[:, R_OUT:R_OUT + FF, :], Wout.rearrange("p (n k) -> p n k", k=P)).then_inc(S["w_in_b"], 16)
            sp.dma_start(raw[:, R_WI:R_WI + EXPERTS, :], Wi.rearrange("e d h -> d e h")).then_inc(S["w_in_c"], 16)
            sp.dma_start(raw_xq[:], xWq).then_inc(S["w_in_c"], 16)
            sp.dma_start(raw_xk[:], xWk).then_inc(S["w_in_c"], 16)
            sp.dma_start(wmo_sb[:], Wmo.rearrange("e h d -> h e d")).then_inc(S["w_in_c"], 16)
            sp.dma_start(wr_sb[:], Wr).then_inc(S["w_in_c"], 16)
            sp.dma_start(mask_sb[:], mask).then_inc(S["w_in_c"], 16)
            sp.dma_start(xbv_sb[:], xbv.rearrange("(a n) -> a n", a=1).to_broadcast([P, P])).then_inc(S["w_in_c"], 16)

            def ctx_load(k, b):
                after_all(sp, ("ctx_T_ps", k))
                sp.dma_start(ctx_sb[:, b, :], ctx[k]).then_inc(S["ctx_in"], 16)

            def parts_save(k, b):
                after_all(sp, ("q_stacked", 16 * k))
                after_all(sp, ("qkv_hi", k + 1))
                after_all(sp, ("qkv_mid", k + 1))
                after_all(sp, ("qkv_lo", k + 1))
                sp.dma_start(scratch[b, 0:2 * PARTS].rearrange("c r s -> r c s"),
                             qk_parts[:, b].rearrange("p a c s -> p (a c) s")).then_inc(S["parts_saved"], 16)
                sp.dma_start(scratch[b, 2 * PARTS:3 * PARTS - 1].rearrange("c r s -> r c s"),
                             qk_parts[:, b, 1, 0:PARTS - 1]).then_inc(S["parts_saved"], 16)

            def parts_stack(k, b):
                after_all(sp, ("parts_saved", 32 * (k + 1)))
                after_all(sp, ("att_scores_ps", 4 * (k - 1)))
                after_all(sp, ("max_scores_ps", 4 * k))
                rot = scratch[b, PARTS:2 * PARTS]
                rot = bass.AP(rot.tensor, rot.offset, [[P * P, PARTS], [HEADS * P, PARTS * HD], [1, HEADS * P]])
                sp.dma_start(q_stack[0:QROWS, b, :, :], rot).then_inc(S["q_stacked"], 16)
                rep = scratch[b, 0:PARTS]
                rep = bass.AP(rep.tensor, rep.offset, [[0, PARTS], [HEADS * P, PARTS * HD], [1, HEADS * P]])
                sp.dma_start(k_stack[0:QROWS, b, :, :], rep).then_inc(S["k_stacked"], 16)

            def max_stack(k, b):
                after_all(sp, ("max_mT", k + 1))
                after_all(sp, ("att_scores_ps", 4 * k))
                sp.dma_start(q_stack[QROWS:SROWS, b, :, :], nmT[:, :]).then_inc(S["m_stacked"], 16)

            def store(k, b):
                after_all(sp, ("moe_out", k + 1))
                sp.dma_start(out[k], out_sb[:, b, :]).then_inc(S["stored"], 16)

            def step(t, par):
                run(t, par, 3, max_stack)
                run(t, par, 2, parts_stack)
                run(t, par, 3, ctx_load)
                run(t, par, 1, parts_save)
                run(t, par, 8, store)

            sp.wait_ge(S["const_dve"], 5)
            steps(sp, step)
            sp.wait_ge(S["stored"], 16 * TILES)

        @block.gpsimd
        def _(pool):
            nc.gpsimd.memset(ident[:], 0.0).then_inc(S["const_pool"], 1)
            nc.gpsimd.memset(above[:], 0.0).then_inc(S["const_pool"], 1)
            nc.gpsimd.memset(below[:], 0.0).then_inc(S["const_pool"], 1)
            nc.gpsimd.memset(neghalf[:], -0.5).then_inc(S["const_pool"], 1)
            pool.wait_ge(S["const_pool"], 4)
            nc.gpsimd.affine_select(out=ident[:], in_=ident[:], compare_op=ALU.not_equal, fill=1.0, base=0,
                                    pattern=[[-1, P]], channel_multiplier=1).then_inc(S["const_pool"], 1)
            nc.gpsimd.affine_select(out=above[:], in_=above[:], compare_op=ALU.is_ge, fill=MASKED, base=0,
                                    pattern=[[0, 4], [-1, P]], channel_multiplier=1).then_inc(S["const_pool"], 1)
            nc.gpsimd.affine_select(out=below[:], in_=below[:], compare_op=ALU.is_ge, fill=MASKED, base=0,
                                    pattern=[[0, 4], [1, P]], channel_multiplier=-1).then_inc(S["const_pool"], 1)
            pool.wait_ge(S["const_pool"], 7)
            nc.gpsimd.tensor_copy(identb[:], ident[:]).then_inc(S["const_pool"], 1)

            def power(src, dst, ready, n, mean, rsd, scale, eps, tmp, used):
                after_all(pool, (ready, n), (used, n - 1))
                nc.gpsimd.tensor_scalar(tmp, src, scale, eps, ALU.mult, ALU.add).then_inc(S[mean], 1)
                after(pool, mean, n)
                nc.gpsimd.tensor_tensor(dst, tmp, neghalf[:], ALU.pow).then_inc(S[rsd], 1)

            def gru_power(k, b):
                power(ss[:, 0:1], rs[:, 0:1], "gru_ss", k + 1, "gru_ms", "gru_rs", 1.0 / P, RMS_EPS, ms[:, 0:1], "gru_xn")

            def qkv_power(k, b):
                power(ss[:, 1:2], rs[:, 1:2], "qkv_ss", k + 1, "qkv_ms", "qkv_rs", 1.0 / P, RMS_EPS, ms[:, 1:2], "qkv_xn")

            def ffn_power(k, b):
                power(ss[:, 2:3], rs[:, 2:3], "ffn_ss", k + 1, "ffn_ms", "ffn_rs", 1.0 / P, RMS_EPS, ms[:, 2:3], "ffn_xn")

            def ffn_ln_power(k, b):
                power(mv[:, 0, 1:2], lrs[:, 0:1], "ffn_mv", k + 1, "ffn_ve", "ffn_rs1", 1.0, LN_EPS, ve[:, 0:1], "ffn_y1")

            def xat_ln_power(k, b):
                power(mv[:, 1, 1:2], lrs[:, 1:2], "xat_mv", k + 1, "xat_ve", "xat_rs", 1.0, LN_EPS, ve[:, 1:2], "xat_y2")

            def moe_ln_power(k, b):
                power(mv[:, 2, 1:2], lrs[:, 2:3], "moe_mv", k + 1, "moe_ve", "moe_rs", 1.0, LN_EPS, ve[:, 2:3], "moe_out")

            def gru_decay(k, b):
                after_all(pool, ("gru_tanh", k + 1), ("gru_scan", k))
                nc.gpsimd.tensor_scalar(gru_a[:], gru_t[:, 2, :], 0.499, 0.5, ALU.mult, ALU.add).then_inc(S["gru_decay"], 1)

            def ffn_residual(k, b):
                after(pool, "att_x2", k + 1)
                after(pool, "ffn_z", k)
                nc.gpsimd.tensor_tensor(x02[:], x_all[:, k, :], x2[:, b, :], ALU.add).then_inc(S["ffn_x02"], 1)

            def xat_residual(k, b):
                after(pool, "ffn_y1", k + 1)
                after(pool, "xat_z", k)
                nc.gpsimd.tensor_tensor(y1b[:], y1[:, b, :], xbv_sb[:], ALU.add).then_inc(S["xat_y1b"], 1)

            def max_split(k, b):
                after_all(pool, ("max_max", 4 * (k + 1)), ("max_mT_ps", k))
                nc.gpsimd.tensor_copy(nm_parts[:, 0, :], neg_max[:]).then_inc(S["max_n1"], 1)
                after(pool, "max_n1", k + 1)
                nc.gpsimd.tensor_tensor(nm_rest[:], neg_max[:], nm_parts[:, 0, :], ALU.subtract).then_inc(S["max_r1"], 1)
                after_all(pool, ("max_r1", k + 1))
                nc.gpsimd.tensor_copy(nm_parts[:, 1, :], nm_rest[:]).then_inc(S["max_n2"], 1)
                after(pool, "max_n2", k + 1)
                nc.gpsimd.tensor_tensor(nm_parts[:, 2, :], nm_rest[:], nm_parts[:, 1, :], ALU.subtract).then_inc(S["max_n3"], 1)

            def qk_low(k, b):
                after(pool, "qkv_mid", k + 1)
                after(pool, "parts_saved", 32 * (k - 1))
                nc.gpsimd.tensor_tensor(qk_parts[:, b, :, 2, :], qk_rest[:], qk_parts[:, b, :, 1, :], ALU.subtract).then_inc(S["qkv_lo"], 1)

            def step(t, par):
                run(t, par, 5, ffn_power)
                run(t, par, 5, ffn_residual)
                run(t, par, 0, gru_power)
                run(t, par, 6, ffn_ln_power)
                run(t, par, 1, qkv_power)
                run(t, par, 7, xat_ln_power)
                run(t, par, 8, moe_ln_power)
                run(t, par, 6, xat_residual)
                run(t, par, 3, max_split)
                run(t, par, 1, qk_low)
                run(t, par, 0, gru_decay)

            steps(pool, step)

        @block.tensor
        def _(pe):
            homes = [ps_scores[:], ps_probs[:], banks[4][:], banks[5][:], banks[0][:], banks[1][:], banks[2][:]]
            pe.wait_ge(S["const_pool"], 8)
            for g in range(NRAW // 4):
                if g == 0:
                    pe.wait_ge(S["w_in_a"], 160)
                if g == 1:
                    pe.wait_ge(S["w_in_b"], 80)
                if g == 5:
                    pe.wait_ge(S["w_in_c"], 112)
                for n in range(4):
                    last = nc.tensor.transpose(homes[g][:, n, :], raw[:, 4 * g + n, :], ident[:])
                last.then_inc(S["w_ps"], 1)
            nc.tensor.matmul(banks[3][:, 0, :], raw_xk[:], raw_xq[:], start=True, stop=True).then_inc(S["w_ps"], 1)
            pe.wait_ge(S["w_act"], 4)
            pe.wait_ge(S["w_dve"], 8)
            for e in range(EXPERTS):
                last = nc.tensor.matmul(banks[4 + e // 4][:, e % 4, :], wiT[:, e, :], wmo_sb[:, e, :], start=True, stop=True)
            last.then_inc(S["w_ps"], 1)
            pe.wait_ge(S["w_act"], 5)
            pe.wait_ge(S["const_dve"], 5)

            def turn(fill, k, src, done):
                bank_free(pe, k, fill)
                nc.tensor.transpose(view(fill)[:, 0, :], src, ident[:]).then_inc(S[done], 1)

            def gru_turn(k, b):
                after(pe, "gru_xn", k + 1)
                turn("gru_turn", k, xn[:, 0, :], "gru_xT_ps")

            def gru_gates(k, b):
                after(pe, "gru_xT", k + 1)
                bank_free(pe, k, "gru_gates")
                for n in range(3):
                    last = nc.tensor.matmul(view("gru_gates")[:, n, :], gruT[:, n, :], xT[:, 0, :], start=True, stop=True)
                last.then_inc(S["gru_gates_ps"], 1)

            def gru_turn_back(k, b):
                after(pe, "gru_scan", k + 1)
                turn("gru_turn_back", k, gru_h[:], "gru_hT_ps")

            def qkv_turn(k, b):
                after(pe, "qkv_xn", k + 1)
                turn("qkv_turn", k, xn[:, 1, :], "qkv_xT_ps")

            def qk_project(k, b):
                after(pe, "qkv_xT", k + 1)
                bank_free(pe, k, "qk_project")
                for n in range(2):
                    last = nc.tensor.matmul(view("qk_project")[:, n, :], qkvT[:, n, :], qkv_xT[:, b, :], start=True, stop=True)
                last.then_inc(S["qkv_ps"], 1)

            def v_project(k, b):
                after(pe, "qkv_xT", k + 1)
                bank_free(pe, k, "v_project")
                nc.tensor.matmul(view("v_project")[:, 0, :], qkv_xT[:, b, :], qkvT[:, 2, :], start=True, stop=True).then_inc(S["max_v_ps"], 1)

            def scores(k, b, n):
                if n == 0:
                    after(pe, "q_stacked", 16 * (k + 1))
                    after(pe, "k_stacked", 16 * (k + 1))
                after(pe, "max_max", 4 * k + n)
                for h in range(QUARTER):
                    nc.tensor.matmul(ps_scores[:, h, :], q_stack[0:QROWS, b, QUARTER * n + h, :],
                                     k_stack[0:QROWS, b, QUARTER * n + h, :], start=(h == 0), stop=False)
                nc.tensor.matmul(ps_scores[:], identb[:], above[:], start=False, stop=True).then_inc(S["max_scores_ps"], 1)

            def max_turn(k, b):
                after_all(pe, ("max_n3", k + 1), last_use(k, "max_turn"))
                nc.tensor.transpose(view("max_turn")[0:PARTS * HEADS, 0, 0:P // 2].bitcast(BF16),
                                    nm_parts[:].rearrange("p c h -> p (c h)"), identb[:]).then_inc(S["max_mT_ps"], 1)

            def scores_turned(k, b, n):
                if n == 0:
                    after(pe, "m_stacked", 16 * (k + 1))
                after(pe, "att_p", 4 * k + n)
                for h in range(QUARTER):
                    nc.tensor.matmul(ps_probs[:, h, :], k_stack[0:SROWS, b, QUARTER * n + h, :],
                                     q_stack[0:SROWS, b, QUARTER * n + h, :], start=(h == 0), stop=False)
                nc.tensor.matmul(ps_probs[:], identb[:], below[:], start=False, stop=True).then_inc(S["att_scores_ps"], 1)

            def att_values(k, b):
                after(pe, "max_v", k + 1)
                after(pe, "att_p", 4 * (k + 1))
                bank_free(pe, k, "att_values")
                for h in range(HEADS):
                    last = nc.tensor.matmul(o_view()[:, h, :], probs[:, h // QUARTER, h % QUARTER, :],
                                            values[:, b, h, :], start=True, stop=True)
                last.then_inc(S["att_o_ps"], 1)

            def att_turn(k, b):
                after(pe, "att_o", k + 1)
                turn("att_turn", k, att_o[:], "att_oT_ps")

            def att_project(k, b):
                after(pe, "att_oT", k + 1)
                bank_free(pe, k, "att_project")
                nc.tensor.matmul(view("att_project")[:, 0, :], att_oT[:], woT[:], start=True, stop=True).then_inc(S["att_y_ps"], 1)

            def ffn_turn(k, b):
                after(pe, "ffn_xn", k + 1)
                turn("ffn_turn", k, xn[:, 2, :], "ffn_xT_ps")

            def ffn_hidden(k, b, fill, g, done):
                after(pe, "ffn_xT", k + 1)
                bank_free(pe, k, fill)
                for n in range(FF):
                    last = nc.tensor.matmul(view(fill)[:, n, :], guT[:, g, n * P:(n + 1) * P], xT[:, 1, :], start=True, stop=True)
                last.then_inc(S[done], 1)

            def ffn_gate(k, b):
                ffn_hidden(k, b, "ffn_gate", 0, "ffn_gate_ps")

            def ffn_up(k, b):
                ffn_hidden(k, b, "ffn_up", 1, "ffn_up_ps")

            def ffn_down(k, b):
                after(pe, "ffn_h", k + 1)
                bank_free(pe, k, "ffn_down")
                for n in range(FF):
                    last = nc.tensor.matmul(view("ffn_down")[:, 0, :], hidden[:, n, :], outT[:, n, :], start=(n == 0), stop=(n == FF - 1))
                last.then_inc(S["ffn_y_ps"], 1)

            def ctx_turn(k, b):
                after(pe, "ctx_in", 16 * (k + 1))
                turn("ctx_turn", k, ctx_sb[:, b, :], "ctx_T_ps")

            def ctx_project(k, b):
                after(pe, "ctx_T", k + 1)
                bank_free(pe, k, "ctx_project")
                nc.tensor.matmul(view("ctx_project")[:, 0, :], w_kq[:], ctxT[:], start=True, stop=True)
                nc.tensor.matmul(view("ctx_project")[:, 1, :], ctxT[:], xwvT[:], start=True, stop=True).then_inc(S["ctx_kv_ps"], 1)

            def xat_turn(k, b):
                after(pe, "ffn_y1", k + 1)
                turn("xat_turn", k, y1[:, b, :], "xat_xT_ps")

            def xat_scores(k, b):
                after(pe, "xat_xT", k + 1)
                after(pe, "ctx_kv", k + 1)
                bank_free(pe, k, "xat_scores")
                nc.tensor.matmul(view("xat_scores")[:, 0, :], y1T[:], ctx_kv[:, b, 0, :], start=True, stop=True).then_inc(S["xat_s_ps"], 1)

            def xat_turn_probs(k, b):
                after(pe, "xat_p", k + 1)
                turn("xat_turn_probs", k, xat_p[:], "xat_pT_ps")

            def xat_values(k, b):
                after(pe, "xat_pT", k + 1)
                bank_free(pe, k, "xat_values")
                nc.tensor.matmul(view("xat_values")[:, 0, :], xat_pT[:], ctx_kv[:, b, 1, :], start=True, stop=True).then_inc(S["xat_y_ps"], 1)

            def moe_turn(k, b):
                after(pe, "xat_y2", k + 1)
                turn("moe_turn", k, y2[:, b, :], "moe_xT_ps")

            def moe_logits(k, b):
                after(pe, "moe_xT", k + 1)
                bank_free(pe, k, "moe_logits")
                nc.tensor.matmul(view("moe_logits")[:, 0, 0:EXPERTS], y2T[:], wr_sb[:], start=True, stop=True).then_inc(S["moe_logits_ps"], 1)

            def moe_experts(k, b, n):
                fill = ("moe_experts_0", "moe_experts_1")[n]
                after(pe, "moe_xT", k + 1)
                bank_free(pe, k, fill)
                nc.tensor.matmul(as_one(view(fill)), y2T[:], w_moe[:, 4 * n:4 * n + 4, :], start=True, stop=True).then_inc(S[("moe_m0_ps", "moe_m1_ps")[n]], 1)

            def step(t, par):
                run(t, par, 5, ctx_turn)
                run(t, par, 2, qkv_turn)
                run(t, par, 5, scores_turned, 3)
                run(t, par, 4, scores, 1)
                run(t, par, 2, qk_project)
                run(t, par, 7, xat_turn)
                run(t, par, 5, att_values)
                run(t, par, 4, scores, 2)
                run(t, par, 6, ffn_up)
                run(t, par, 4, scores, 3)
                run(t, par, 8, moe_turn)
                run(t, par, 5, att_turn)
                run(t, par, 7, xat_scores)
                run(t, par, 8, moe_logits)
                run(t, par, 1, gru_gates)
                run(t, par, 5, att_project)
                run(t, par, 4, max_turn)
                run(t, par, 6, ffn_down)
                run(t, par, 8, moe_experts, 0)
                run(t, par, 7, xat_turn_probs)
                run(t, par, 5, ctx_project)
                run(t, par, 1, gru_turn_back)
                run(t, par, 3, v_project)
                run(t, par, 5, ffn_turn)
                run(t, par, 7, xat_values)
                run(t, par, 4, scores_turned, 0)
                run(t, par, 8, moe_experts, 1)
                run(t, par, 4, scores_turned, 1)
                run(t, par, 5, ffn_gate)
                run(t, par, 4, scores_turned, 2)
                run(t, par, 3, scores, 0)
                run(t, par, 0, gru_turn)

            steps(pe, step)

        @block.scalar
        def _(act):
            act.wait_ge(S["w_in_a"], 160)
            act.wait_ge(S["w_ps"], 3)
            nc.scalar.activation(guT[:, 0, :], as_one(banks[4][:]), ACT.Copy, scale=cols[:, 2:3]).then_inc(S["w_act"], 1)
            act.wait_ge(S["w_ps"], 4)
            nc.scalar.activation(guT[:, 1, :], as_one(banks[5][:]), ACT.Copy, scale=cols[:, 2:3]).then_inc(S["w_act"], 1)
            act.wait_ge(S["w_ps"], 5)
            nc.scalar.activation(outT[:], banks[0][:], ACT.Copy, scale=0.5).then_inc(S["w_act"], 1)
            act.wait_ge(S["w_ps"], 6)
            nc.scalar.copy(wiT[:, 0:4, :], banks[1][:]).then_inc(S["w_act"], 1)
            act.wait_ge(S["w_ps"], 9)
            nc.scalar.copy(w_moe[:, 0:4, :], banks[4][:])
            nc.scalar.copy(w_moe[:, 4:8, :], banks[5][:]).then_inc(S["w_act"], 1)

            def squares(src, n, done):
                nc.scalar.activation(junk[:, n, :], src, ACT.Square, accum_out=ss[:, n:n + 1]).then_inc(S[done], 1)

            def normalize(k, src, n, rsd, done, used):
                after_all(act, (rsd, k + 1), (used, k))
                nc.scalar.activation(xn[:, n, :], src, ACT.Copy, scale=rs[:, n:n + 1]).then_inc(S[done], 1)

            def gru_squares(k, b):
                after_all(act, ("gru_ms", k))
                squares(x_all[:, k, :], 0, "gru_ss")

            def gru_normalize(k, b):
                normalize(k, x_all[:, k, :], 0, "gru_rs", "gru_xn", "gru_xT_ps")

            def gru_copy(k, b):
                after(act, "gru_xT_ps", k + 1)
                after(act, "gru_gates_ps", k)
                nc.scalar.copy(xT[:, 0, :], view("gru_turn")[:, 0, :]).then_inc(S["gru_xT"], 1)

            def gru_tanh(k, b):
                after(act, "gru_gates_ps", k + 1)
                after(act, "gru_xs", k)
                after(act, "gru_decay", k)
                gates = view("gru_gates")
                nc.scalar.activation(gru_t[:, 0, :], gates[:, 0, :], ACT.Tanh, bias=half_b[:, 0:1], scale=0.5)
                nc.scalar.activation(gru_t[:, 1, :], gates[:, 1, :], ACT.Tanh, bias=cols[:, 4:5])
                nc.scalar.activation(gru_t[:, 2, :], gates[:, 2, :], ACT.Tanh, bias=half_b[:, 1:2], scale=0.5).then_inc(S["gru_tanh"], 1)

            def qkv_squares(k, b):
                after_all(act, ("gru_x1", k + 1), ("qkv_ms", k))
                squares(x1_all[:, k, :], 1, "qkv_ss")

            def qkv_normalize(k, b):
                normalize(k, x1_all[:, k, :], 1, "qkv_rs", "qkv_xn", "qkv_xT_ps")

            def qkv_copy(k, b):
                after(act, "qkv_xT_ps", k + 1)
                after(act, "max_v_ps", k - 1)
                after(act, "qkv_ps", k - 1)
                nc.scalar.copy(qkv_xT[:, b, :], view("qkv_turn")[:, 0, :]).then_inc(S["qkv_xT"], 1)

            def qk_high(k, b):
                after(act, "qkv_ps", k + 1)
                after(act, "parts_saved", 32 * (k - 1))
                nc.scalar.copy(qk_parts[:, b, :, 0, :], view("qk_project")[:, 0:2, :]).then_inc(S["qkv_hi"], 1)

            def qk_middle(k, b):
                after(act, "qkv_rest", k + 1)
                nc.scalar.copy(qk_parts[:, b, :, 1, :], qk_rest[:]).then_inc(S["qkv_mid"], 1)

            def v_copy(k, b):
                after(act, "max_v_ps", k + 1)
                after(act, "att_o_ps", k - 1)
                nc.scalar.copy(values[:, b, :, 0:HD], view("v_project")[:, 0, :].rearrange("p (h d) -> p h d", h=HEADS)).then_inc(S["max_v"], 1)

            def max_copy(k, b):
                after(act, "max_mT_ps", k + 1)
                after(act, "m_stacked", 16 * k)
                nc.scalar.copy(nmT[:], view("max_turn")[0:PARTS * HEADS, 0, 0:P // 2].bitcast(BF16)).then_inc(S["max_mT"], 1)

            def exponentials(k, b, n):
                after(act, "att_scores_ps", 4 * k + n + 1)
                after(act, "att_o_ps", k)
                nc.scalar.activation(probs[:, n, :, :], ps_probs[:], ACT.Exp, scale=HD ** -0.5).then_inc(S["att_p"], 1)

            def att_copy(k, b):
                after(act, "att_oT_ps", k + 1)
                after(act, "att_y_ps", k)
                nc.scalar.copy(att_oT[:], view("att_turn")[:, 0, :]).then_inc(S["att_oT"], 1)

            def ffn_squares(k, b):
                after(act, "att_x2", k + 1)
                after(act, "ffn_ms", k)
                squares(x2[:, b, :], 2, "ffn_ss")

            def ffn_normalize(k, b):
                normalize(k, x2[:, b, :], 2, "ffn_rs", "ffn_xn", "ffn_xT_ps")

            def ffn_copy(k, b):
                after(act, "ffn_xT_ps", k + 1)
                after(act, "ffn_gate_ps", k)
                after(act, "ffn_up_ps", k)
                nc.scalar.copy(xT[:, 1, :], view("ffn_turn")[:, 0, :]).then_inc(S["ffn_xT"], 1)

            def ffn_tanh(k, b):
                after(act, "ffn_gate_ps", k + 1)
                after(act, "ffn_t1", k)
                nc.scalar.activation(gate_t[:], as_one(view("ffn_gate")), ACT.Tanh, scale=0.5).then_inc(S["ffn_tanh"], 1)

            def ctx_copy(k, b):
                after(act, "ctx_T_ps", k + 1)
                after(act, "ctx_kv_ps", k)
                nc.scalar.copy(ctxT[:], view("ctx_turn")[:, 0, :]).then_inc(S["ctx_T"], 1)

            def ctx_copy_kv(k, b):
                after(act, "ctx_kv_ps", k + 1)
                after(act, "xat_y_ps", k - 1)
                nc.scalar.copy(ctx_kv[:, b, :, :], view("ctx_project")[:, 0:2, :]).then_inc(S["ctx_kv"], 1)

            def xat_copy(k, b):
                after(act, "xat_xT_ps", k + 1)
                after(act, "xat_s_ps", k)
                nc.scalar.copy(y1T[:], view("xat_turn")[:, 0, :]).then_inc(S["xat_xT"], 1)

            def xat_exp(k, b):
                after(act, "xat_negm", k + 1)
                after(act, "xat_pT_ps", k)
                after(act, "xat_rd", k)
                nc.scalar.activation(xat_p[:], xat_s[:], ACT.Exp, bias=xat_m[:, 1:2],
                                     accum_out=xat_l[:, 0:1]).then_inc(S["xat_p"], 1)

            def xat_copy_probs(k, b):
                after(act, "xat_pT_ps", k + 1)
                after(act, "xat_y_ps", k)
                nc.scalar.copy(xat_pT[:], view("xat_turn_probs")[:, 0, :]).then_inc(S["xat_pT"], 1)

            def moe_copy(k, b):
                after(act, "moe_xT_ps", k + 1)
                after(act, "moe_logits_ps", k)
                after(act, "moe_m0_ps", k)
                after(act, "moe_m1_ps", k)
                nc.scalar.copy(y2T[:], view("moe_turn")[:, 0, :]).then_inc(S["moe_xT"], 1)

            def moe_copy_logits(k, b):
                after(act, "moe_logits_ps", k + 1)
                after(act, "moe_c", k)
                nc.scalar.copy(moe_lg[:], view("moe_logits")[:, 0, 0:EXPERTS]).then_inc(S["moe_lg"], 1)

            def moe_exp(k, b):
                after(act, "moe_negm", k + 1)
                after(act, "moe_c", k)
                nc.scalar.activation(moe_e[:], moe_lg[:], ACT.Exp, bias=moe_m[:, 0:1],
                                     accum_out=moe_l[:, 0:1]).then_inc(S["moe_e"], 1)

            def step(t, par):
                run(t, par, 1, gru_squares)
                run(t, par, 6, ffn_copy)
                run(t, par, 4, v_copy)
                run(t, par, 5, exponentials, 0)
                run(t, par, 2, qkv_squares)
                run(t, par, 1, gru_normalize)
                run(t, par, 5, exponentials, 1)
                run(t, par, 2, qkv_normalize)
                run(t, par, 6, ctx_copy_kv)
                run(t, par, 5, exponentials, 2)
                run(t, par, 6, ffn_tanh)
                run(t, par, 2, qkv_copy)
                run(t, par, 5, ctx_copy)
                run(t, par, 5, exponentials, 3)
                run(t, par, 1, gru_copy)
                run(t, par, 2, qk_high)
                run(t, par, 2, qk_middle)
                run(t, par, 7, xat_copy)
                run(t, par, 8, moe_copy)
                run(t, par, 5, att_copy)
                run(t, par, 8, moe_copy_logits)
                run(t, par, 1, gru_tanh)
                run(t, par, 4, max_copy)
                run(t, par, 5, ffn_squares)
                run(t, par, 8, moe_exp)
                run(t, par, 7, xat_exp)
                run(t, par, 5, ffn_normalize)
                run(t, par, 7, xat_copy_probs)

            act.wait_ge(S["const_dve"], 5)
            act.wait_ge(S["x_in"], 32)
            steps(act, step)

        @block.vector
        def _(dve):
            nc.vector.memset(q_stack[:], 1.0).then_inc(S["const_dve"], 1)
            nc.vector.memset(k_stack[:], 1.0).then_inc(S["const_dve"], 1)
            nc.vector.memset(values[:], 1.0).then_inc(S["const_dve"], 1)
            nc.vector.memset(ones8[:], 1.0).then_inc(S["const_dve"], 1)
            dve.wait_ge(S["w_in_a"], 160)
            dve.wait_ge(S["w_ps"], 1)
            nc.vector.tensor_scalar(gruT[:], ps_scores[:, 0:3, :], cols[:, 0:1], None, ALU.mult).then_inc(S["w_dve"], 1)
            nc.vector.tensor_copy(woT[:], ps_scores[:, 3, :]).then_inc(S["w_dve"], 1)
            nc.vector.tensor_scalar(half_b[:, 0:1], cols[:, 3:4], 0.5, None, ALU.mult)
            nc.vector.tensor_scalar(half_b[:, 1:2], cols[:, 5:6], 0.5, None, ALU.mult).then_inc(S["const_dve"], 1)
            dve.wait_ge(S["w_ps"], 2)
            for n in range(2):
                nc.vector.tensor_scalar(qkvT[:, n, :].rearrange("p (d h) -> p h d", d=HD),
                                        ps_probs[:, 1 - n, :].rearrange("p (h d) -> p h d", d=HD),
                                        cols[:, 1:2], None, ALU.mult).then_inc(S["w_dve"], 1)
            nc.vector.tensor_scalar(qkvT[:, 2, :], ps_probs[:, 2, :], cols[:, 1:2], None, ALU.mult).then_inc(S["w_dve"], 1)
            nc.vector.tensor_copy(xwvT[:], ps_probs[:, 3, :]).then_inc(S["w_dve"], 1)
            dve.wait_ge(S["w_ps"], 7)
            nc.vector.tensor_copy(wiT[:, 4:8, :], banks[2][:]).then_inc(S["w_dve"], 1)
            dve.wait_ge(S["w_ps"], 8)
            nc.vector.tensor_scalar(w_kq[:], banks[3][:, 0, :], P ** -0.5, None, ALU.mult).then_inc(S["w_dve"], 1)

            def layernorm_apply(n, k, src, dst, rsd, done):
                after(dve, rsd, k + 1)
                nc.vector.tensor_scalar(dst, src, mv[:, n, 0:1], lrs[:, n:n + 1], ALU.subtract, ALU.mult).then_inc(S[done], 1)

            def gru_input(k, b):
                after(dve, "gru_tanh", k + 1)
                after(dve, "gru_scan", k)
                nc.vector.scalar_tensor_tensor(gru_xs[:], gru_t[:, 0, :], 1.0, gru_t[:, 1, :], ALU.add, ALU.mult).then_inc(S["gru_xs"], 1)

            def gru_scan(k, b):
                after(dve, "gru_xs", k + 1)
                after(dve, "gru_decay", k + 1)
                after(dve, "gru_hT_ps", k)
                nc.vector.tensor_tensor_scan(gru_h[:], gru_a[:], gru_xs[:], 0.0, ALU.mult, ALU.add).then_inc(S["gru_scan"], 1)

            def gru_out(k, b):
                after(dve, "gru_hT_ps", k + 1)
                nc.vector.scalar_tensor_tensor(x1_all[:, k, :], view("gru_turn_back")[:, 0, :], 0.5, x_all[:, k, :],
                                               ALU.mult, ALU.add).then_inc(S["gru_x1"], 1)

            def qk_rest_of(k, b):
                after(dve, "qkv_hi", k + 1)
                after(dve, "qkv_lo", k)
                nc.vector.tensor_tensor(qk_rest[:], view("qk_project")[:, 0:2, :], qk_parts[:, b, :, 0, :],
                                        ALU.subtract).then_inc(S["qkv_rest"], 1)

            def maxima(k, b, n):
                after(dve, "max_scores_ps", 4 * k + n + 1)
                if n == 0:
                    after(dve, "max_n3", k)
                nc.vector.tensor_reduce(neg_max[:, QUARTER * n:QUARTER * n + QUARTER], ps_scores[:], AX_X,
                                        ALU.max, negate=True).then_inc(S["max_max"], 1)

            def att_reciprocal(k, b):
                after(dve, "att_o_ps", k + 1)
                after(dve, "att_o", k)
                nc.vector.reciprocal(att_rd[:], o_view()[:, :, HD]).then_inc(S["att_rd"], 1)

            def att_divide(k, b):
                after(dve, "att_rd", k + 1)
                after(dve, "att_oT_ps", k)
                nc.vector.tensor_tensor(att_o[:].rearrange("p (h d) -> p h d", h=HEADS), o_view()[:, :, 0:HD],
                                        att_rd[:].unsqueeze(2).to_broadcast([P, HEADS, HD]), ALU.mult).then_inc(S["att_o"], 1)

            def att_out(k, b):
                after(dve, "att_y_ps", k + 1)
                after(dve, "ffn_x02", k - 1)
                after(dve, "ffn_xn", k - 1)
                nc.vector.tensor_tensor(x2[:, b, :], view("att_project")[:, 0, :], x1_all[:, k, :], ALU.add).then_inc(S["att_x2"], 1)

            def ffn_silu(k, b):
                after(dve, "ffn_tanh", k + 1)
                after(dve, "ffn_h", k)
                nc.vector.scalar_tensor_tensor(gate_1[:], gate_t[:], 1.0, as_one(view("ffn_gate")), ALU.add, ALU.mult).then_inc(S["ffn_t1"], 1)

            def ffn_product(k, b):
                after(dve, "ffn_t1", k + 1)
                after(dve, "ffn_up_ps", k + 1)
                after(dve, "ffn_y_ps", k)
                nc.vector.tensor_tensor(hidden[:].rearrange("p a b -> p (a b)"), gate_1[:], as_one(view("ffn_up")), ALU.mult).then_inc(S["ffn_h"], 1)

            def ffn_out(k, b):
                after(dve, "ffn_y_ps", k + 1)
                after(dve, "ffn_x02", k + 1)
                after(dve, "ffn_y1", k)
                nc.vector.tensor_tensor(z[:, 0, :], view("ffn_down")[:, 0, :], x02[:], ALU.add).then_inc(S["ffn_z"], 1)

            def ffn_stats(k, b):
                after(dve, "ffn_z", k + 1)
                after(dve, "ffn_mv", k)
                nc.vector.bn_stats(stats[:, 0, :], z[:, 0, :]).then_inc(S["ffn_stats"], 1)

            def ffn_moments(k, b):
                after_all(dve, ("ffn_stats", k + 1), ("ffn_y1", k))
                nc.vector.bn_aggr(mv[:, 0, :], stats[:, 0, :]).then_inc(S["ffn_mv"], 1)

            def ffn_layernorm(k, b):
                after(dve, "xat_xT_ps", k - 1)
                after(dve, "xat_y1b", k - 1)
                layernorm_apply(0, k, z[:, 0, :], y1[:, b, :], "ffn_rs1", "ffn_y1")

            def xat_add_mask(k, b):
                after_all(dve, ("xat_s_ps", k + 1), ("xat_p", k))
                nc.vector.tensor_tensor_reduce(xat_s[:], view("xat_scores")[:, 0, :], mask_sb[:], 1.0, -3.4e38, ALU.add,
                                               ALU.max, xat_m[:, 0:1]).then_inc(S["xat_sm"], 1)

            def xat_negate(k, b):
                after(dve, "xat_sm", k + 1)
                nc.vector.tensor_scalar(xat_m[:, 1:2], xat_m[:, 0:1], -1.0, None, ALU.mult).then_inc(S["xat_negm"], 1)

            def xat_reciprocal(k, b):
                after(dve, "xat_p", k + 1)
                after(dve, "xat_z", k)
                nc.vector.reciprocal(xat_l[:, 1:2], xat_l[:, 0:1]).then_inc(S["xat_rd"], 1)

            def xat_out(k, b):
                after(dve, "xat_rd", k + 1)
                after(dve, "xat_y_ps", k + 1)
                after(dve, "xat_y1b", k + 1)
                after(dve, "xat_y2", k)
                nc.vector.scalar_tensor_tensor(z[:, 1, :], view("xat_values")[:, 0, :], xat_l[:, 1:2], y1b[:],
                                               ALU.mult, ALU.add).then_inc(S["xat_z"], 1)

            def xat_stats(k, b):
                after(dve, "xat_z", k + 1)
                after(dve, "xat_mv", k)
                nc.vector.bn_stats(stats[:, 1, :], z[:, 1, :]).then_inc(S["xat_stats"], 1)

            def xat_moments(k, b):
                after_all(dve, ("xat_stats", k + 1), ("xat_y2", k))
                nc.vector.bn_aggr(mv[:, 1, :], stats[:, 1, :]).then_inc(S["xat_mv"], 1)

            def xat_layernorm(k, b):
                after(dve, "moe_xT_ps", k - 1)
                after(dve, "moe_low", k - 1)
                layernorm_apply(1, k, z[:, 1, :], y2[:, b, :], "xat_rs", "xat_y2")

            def moe_top(k, b):
                after_all(dve, ("moe_lg", k + 1), ("moe_c", k))
                nc.vector.max(top[:], moe_lg[:]).then_inc(S["moe_top"], 1)
                after(dve, "moe_top", k + 1)
                nc.vector.tensor_scalar(moe_m[:, 0:1], top[:, 0:1], -1.0, None, ALU.mult).then_inc(S["moe_negm"], 1)

            def moe_choose(k, b):
                after(dve, "moe_top", k + 1)
                after(dve, "moe_c", k)
                nc.vector.tensor_scalar(moe_eq[:], moe_lg[:], top[:, 1:2], None, ALU.is_equal).then_inc(S["moe_eq"], 1)
                nc.vector.tensor_scalar(moe_gt[:], moe_lg[:], top[:, 1:2], None, ALU.is_gt, ALU.add,
                                        accum_out=moe_n[:]).then_inc(S["moe_gt"], 1)
                after(dve, "moe_eq", k + 1)
                nc.vector.tensor_tensor_scan(moe_cum[:], ones8[:], moe_eq[:], 0.0, ALU.mult, ALU.add).then_inc(S["moe_cum"], 1)
                after(dve, "moe_cum", k + 1)
                after(dve, "moe_gt", k + 1)
                nc.vector.tensor_scalar(moe_lt[:], moe_cum[:], moe_n[:], 2.5, ALU.add, ALU.is_lt).then_inc(S["moe_lt"], 1)
                after(dve, "moe_lt", k + 1)
                nc.vector.tensor_tensor(moe_both[:], moe_lt[:], moe_eq[:], ALU.mult).then_inc(S["moe_both"], 1)
                after(dve, "moe_both", k + 1)
                nc.vector.tensor_tensor(moe_sel[:], moe_both[:], moe_gt[:], ALU.add).then_inc(S["moe_sel"], 1)

            def moe_weights(k, b):
                after(dve, "moe_e", k + 1)
                after(dve, "moe_z", k)
                nc.vector.reciprocal(moe_l[:, 1:2], moe_l[:, 0:1]).then_inc(S["moe_rd"], 1)
                after(dve, "moe_sel", k + 1)
                after(dve, "moe_rd", k + 1)
                nc.vector.scalar_tensor_tensor(moe_c[:], moe_sel[:], moe_l[:, 1:2], moe_e[:], ALU.mult, ALU.mult).then_inc(S["moe_c"], 1)

            def moe_mix(k, b, n):
                after(dve, ("moe_m0_ps", "moe_m1_ps")[n], k + 1)
                after(dve, ("moe_c", "moe_low")[n], k + 1)
                if n == 1:
                    after(dve, "moe_out", k)
                for e in range(4 * n, 4 * n + 4):
                    if e % 4:
                        after(dve, "moe_acc", 6 * k + e - n)
                    nc.vector.scalar_tensor_tensor(z[:, 2, :] if e == EXPERTS - 1 else acc[:, e % 2, :],
                                                   view(("moe_experts_0", "moe_experts_1")[n])[:, e % 4, :], moe_c[:, e:e + 1],
                                                   acc[:, (e + 1) % 2, :] if e else y2[:, b, :], ALU.mult,
                                                   ALU.add).then_inc(S["moe_acc" if e % 4 < 3 else ("moe_low", "moe_z")[n]], 1)

            def moe_stats(k, b):
                after(dve, "moe_z", k + 1)
                after(dve, "moe_mv", k)
                nc.vector.bn_stats(stats[:, 2, :], z[:, 2, :]).then_inc(S["moe_stats"], 1)

            def moe_moments(k, b):
                after_all(dve, ("moe_stats", k + 1), ("moe_out", k))
                nc.vector.bn_aggr(mv[:, 2, :], stats[:, 2, :]).then_inc(S["moe_mv"], 1)

            def moe_layernorm(k, b):
                after(dve, "stored", 16 * k)
                layernorm_apply(2, k, z[:, 2, :], out_sb[:, b, :], "moe_rs", "moe_out")

            def step(t, par):
                run(t, par, 8, moe_weights)
                run(t, par, 1, gru_out)
                run(t, par, 6, ffn_stats)
                run(t, par, 7, xat_reciprocal)
                run(t, par, 8, moe_mix, 0)
                run(t, par, 6, ffn_moments)
                run(t, par, 7, xat_out)
                run(t, par, 7, xat_stats)
                run(t, par, 7, xat_moments)
                run(t, par, 8, moe_mix, 1)
                run(t, par, 6, ffn_layernorm)
                run(t, par, 7, xat_layernorm)
                run(t, par, 8, moe_stats)
                run(t, par, 3, maxima, 0)
                run(t, par, 5, ffn_silu)
                run(t, par, 3, maxima, 1)
                run(t, par, 1, qk_rest_of)
                run(t, par, 8, moe_moments)
                run(t, par, 3, maxima, 2)
                run(t, par, 4, att_reciprocal)
                run(t, par, 4, att_divide)
                run(t, par, 3, maxima, 3)
                run(t, par, 5, ffn_product)
                run(t, par, 6, xat_add_mask)
                run(t, par, 7, moe_top)
                run(t, par, 4, att_out)
                run(t, par, 6, xat_negate)
                run(t, par, 7, moe_choose)
                run(t, par, 8, moe_layernorm)
                run(t, par, 5, ffn_out)
                run(t, par, 0, gru_input)
                run(t, par, 0, gru_scan)

            dve.wait_ge(S["x_in"], 32)
            dve.wait_ge(S["w_in_c"], 112)
            steps(dve, step)


_INS = ['x', 'ctx_1024', 'mask_SxS2_fk0', 'L0_attn_w_rms_mix', 'L0_attn_Wg', 'L0_attn_bg', 'L0_attn_Wv',
        'L0_attn_bv', 'L0_attn_Wd', 'L0_attn_bd', 'L0_attn_w_rms_attn', 'L0_attn_Wqkv', 'L0_attn_Wo',
        'L0_attn_w_rms_ffn', 'L0_attn_Wgate', 'L0_attn_Wup', 'L0_attn_Wout', 'L0_xattn_Wq', 'L0_xattn_Wk',
        'L0_xattn_Wv', 'L0_xattn_bv', 'L0_ffn_Wr', 'L0_ffn_Wi', 'L0_ffn_Wo']


def kernel(**inputs):
    import numpy as _np
    import concourse.bacc as _bacc
    from concourse import mybir as _mybir
    from concourse.bass_utils import run_bass_kernel_spmd as _run

    nc = _bacc.Bacc("TRN2", target_bir_lowering=False, num_devices=1)
    arrays, args = {}, []
    for name in _INS:
        a = _np.ascontiguousarray(inputs[name])
        arrays[f"in_{name}_dram"] = a
        args.append(nc.dram_tensor(f"in_{name}_dram", a.shape, _mybir.dt.from_np(a.dtype), kind="ExternalInput").ap())
    shape = inputs["x"].shape
    args.append(nc.dram_tensor("out_0_dram", shape, _mybir.dt.float32, kind="ExternalOutput").ap())
    decoder_layer(nc, *args)
    r = _run(nc, [arrays], core_ids=[0])
    return r.results[0]["out_0_dram"]
```

```python
from contextlib import ExitStack

import concourse.bass as bass
from concourse import mybir

P = 128
HEADS = 16
HD = P // HEADS
EXPERTS = 8
FF = 4
PARTS = 3
PAIRS = PARTS * PARTS
QROWS = PAIRS * HD
SROWS = QROWS + PARTS
TWO_ONES = 1 + 0x3F80 / 2 ** 23
QUARTER = HEADS // 4
RMS_EPS = 1e-6
LN_EPS = 1e-5
MASKED = -1e30

MAX_LAG = 6

USERS = [
    [("qkv_turn", 2, "qkv_xT"),
     ("xat_turn_probs", 5, "xat_pT"),
     ("xat_values", 5, "xat_z"),
     ("gru_gates", 1, "gru_tanh"),
     ("gru_turn_back", 1, "gru_x1")],
    [("xat_scores", 5, "xat_sm"),
     ("qk_project", 2, "qkv_rest"),
     ("ctx_project", 3, "ctx_kv"),
     ("att_values", 3, "att_o")],
    [("ctx_turn", 3, "ctx_T"),
     ("gru_turn", 1, "gru_xT"),
     ("max_turn", 3, "max_mT"),
     ("moe_logits", 5, "moe_lg")],
    [("xat_turn", 5, "xat_xT"),
     ("att_turn", 4, "att_oT"),
     ("att_project", 4, "att_x2"),
     ("ffn_turn", 4, "ffn_xT"),
     ("v_project", 2, "max_v"),
     ("moe_turn", 5, "moe_xT"),
     ("ffn_down", 4, "ffn_z")],
    [("ffn_gate", 4, "ffn_t1"),
     ("moe_experts_0", 5, "moe_low")],
    [("ffn_up", 4, "ffn_h"),
     ("moe_experts_1", 5, "moe_high")],
]
BANK = {piece: n for n, users in enumerate(USERS) for piece, _, _ in users}

ALU = mybir.AluOpType
ACT = mybir.ActivationFunctionType
F32 = mybir.dt.float32
BF16 = mybir.dt.bfloat16
AX_X = mybir.AxisListType.X

TILE_SEMS = """
gru_ss gru_ms gru_rs gru_xn gru_xT_ps gru_xT gru_gates_ps gru_tanh gru_xs gru_decay gru_scan gru_hT_ps gru_x1
qkv_ss qkv_ms qkv_rs qkv_xn qkv_xT_ps qkv_xT qkv_ps qkv_hi qkv_rest qkv_mid qkv_lo
max_scores_ps max_max max_n1 max_r1 max_n2 max_n3 max_mT_ps max_mT max_v_ps max_v
att_scores_ps att_p att_o_ps att_rd att_o att_oT_ps att_oT att_y_ps att_x2
ffn_ss ffn_ms ffn_rs ffn_xn ffn_xT_ps ffn_xT ffn_gate_ps ffn_up_ps ffn_tanh ffn_t1 ffn_h ffn_x02 ffn_y_ps ffn_z
ffn_stats ffn_mv ffn_ve ffn_rs1 ffn_y1 ctx_T_ps ctx_T ctx_kv_ps ctx_kv
xat_xT_ps xat_xT xat_s_ps xat_sm xat_negm xat_p xat_pT_ps xat_pT xat_rd xat_y1b xat_y_ps xat_z
xat_stats xat_mv xat_ve xat_rs xat_y2
moe_xT_ps moe_xT moe_logits_ps moe_top moe_negm moe_e moe_gt moe_eq moe_cum moe_lt moe_both moe_sel moe_rd moe_c moe_lg
moe_m0_ps moe_m1_ps moe_acc moe_low moe_high moe_z moe_stats moe_mv moe_ve moe_rs moe_out
""".split()
DMA_SEMS = "x_first x_in ctx_in w_small w_col_a w_col_b w_in_q w_in_a w_in_b w_in_c parts_saved q_stacked k_stacked m_stacked stored".split()
SETUP_SEMS = "const_pool const_dve w_ps w_dve w_act".split()


def decoder_layer(nc, x, ctx, mask, w_mix, Wg, bg, Wv, bv, Wd, bd, w_attn, Wqkv, Wo, w_ffn, Wgate, Wup,
                  Wout, xWq, xWk, xWv, xbv, Wr, Wi, Wmo, out):
    TILES = x.shape[0]
    LAST = TILES + MAX_LAG
    LOOP = MAX_LAG + 1 + (MAX_LAG + 1) % 2
    assert TILES % 2 == 0 and TILES > LOOP and x.shape[1:] == (P, P)

    with ExitStack() as stack:
        def sb(name, shape, dt=F32):
            return stack.enter_context(nc.sbuf_tensor(name, shape, dt))

        def psum(name, shape, dt=F32):
            return stack.enter_context(nc.psum_tensor(name, shape, dt))

        S = {name: stack.enter_context(nc.semaphore(name)) for name in TILE_SEMS + DMA_SEMS + SETUP_SEMS}

        ps_scores = psum("ps_scores", [P, QUARTER, P])
        ps_probs = psum("ps_probs", [P, QUARTER, P])
        banks = [psum(f"ps_{n}", [P, 4, P]) for n in range(6)]

        def view(fill):
            return banks[BANK[fill]][:]

        def as_one(ap):
            return ap.rearrange("p a b -> p (a b)")

        def o_view():
            return as_one(view("att_values"))[:, 0:HEADS * (HD + 1)].rearrange("p (h e) -> p h e", h=HEADS)

        ident = sb("ident", [P, P])
        identb = sb("identb", [P, P], BF16)
        above = sb("above", [P, 4, P], BF16)
        below = sb("below", [P, 4, P], BF16)
        neghalf = sb("neghalf", [P, 1])
        unused = sb("unused", [P, 1])
        ones8 = sb("ones8", [P, EXPERTS])
        mask_sb = sb("mask_sb", [P, P])
        xbv_sb = sb("xbv_sb", [P, P])
        cols = sb("cols", [P, 6])
        half_b = sb("half_b", [P, 2])
        NRAW = 28
        raw = sb("raw", [P, NRAW, P])
        R_GRU, R_WO, R_QKV, R_XWV, R_GATE, R_UP, R_OUT, R_WI = 0, 3, 4, 7, 8, 12, 16, 20
        raw_xq = sb("raw_xq", [P, P])
        raw_xk = sb("raw_xk", [P, P])
        wr_sb = sb("wr_sb", [P, EXPERTS])
        wmo_sb = sb("wmo_sb", [P, EXPERTS, P])
        gruT = sb("gruT", [P, 3, P])
        woT = sb("woT", [P, P])
        qkvT = sb("qkvT", [P, 3, P])
        xwvT = sb("xwvT", [P, P])
        guT = sb("guT", [P, 2, FF * P])
        outT = sb("outT", [P, FF, P])
        wiT = sb("wiT", [P, EXPERTS, P])
        w_kq = sb("w_kq", [P, P])
        w_moe = sb("w_moe", [P, EXPERTS, P])

        x_all = sb("x_all", [P, TILES, P])
        x1_all = sb("x1_all", [P, TILES, P])
        junk = sb("junk", [P, 3, P])
        ss = sb("ss", [P, 3])
        ms = sb("ms", [P, 3])
        rs = sb("rs", [P, 3])
        xn = sb("xn", [P, 3, P])
        xT = sb("xT", [P, 2, P])
        qkv_xT = sb("qkv_xT", [P, 2, P])
        gru_t = sb("gru_t", [P, 3, P])
        gru_xs = sb("gru_xs", [P, P])
        gru_a = sb("gru_a", [P, P])
        gru_h = sb("gru_h", [P, P])
        qk_rest = sb("qk_rest", [P, 2, P])
        qk_parts = sb("qk_parts", [P, 2, 2, PARTS, P], BF16)
        q_stack = sb("q_stack", [P, 2, HEADS, P], BF16)
        k_stack = sb("k_stack", [P, 2, HEADS, P], BF16)
        neg_max = sb("neg_max", [P, HEADS])
        nm_rest = sb("nm_rest", [P, HEADS])
        nm_parts = sb("nm_parts", [P, PARTS, HEADS], BF16)
        nmT = sb("nmT", [PARTS * HEADS, P], BF16)
        values = sb("values", [P, 2, HEADS, HD + 1])
        probs = sb("probs", [P, 4, QUARTER, P])
        att_rd = sb("att_rd", [P, HEADS])
        att_o = sb("att_o", [P, P])
        att_oT = sb("att_oT", [P, P])
        x2 = sb("x2", [P, 2, P])
        x02 = sb("x02", [P, P])
        gate_t = sb("gate_t", [P, FF * P])
        gate_1 = sb("gate_1", [P, FF * P])
        hidden = sb("hidden", [P, FF, P])
        z = sb("z", [P, 3, P])
        stats = sb("stats", [P, 3, 6])
        mv = sb("mv", [P, 3, 2])
        ve = sb("ve", [P, 3])
        lrs = sb("lrs", [P, 3])
        y1 = sb("y1", [P, 2, P])
        ctx_sb = sb("ctx_sb", [P, 2, P])
        ctxT = sb("ctxT", [P, P])
        ctx_kv = sb("ctx_kv", [P, 2, 2, P])
        y1T = sb("y1T", [P, P])
        xat_s = sb("xat_s", [P, P])
        xat_m = sb("xat_m", [P, 2])
        xat_p = sb("xat_p", [P, P])
        xat_l = sb("xat_l", [P, 2])
        xat_pT = sb("xat_pT", [P, P])
        y1b = sb("y1b", [P, P])
        y2 = sb("y2", [P, 2, P])
        y2T = sb("y2T", [P, P])
        top = sb("top", [P, EXPERTS])
        moe_lg = sb("moe_lg", [P, EXPERTS])
        moe_m = sb("moe_m", [P, 2])
        moe_e = sb("moe_e", [P, EXPERTS])
        moe_l = sb("moe_l", [P, 2])
        moe_gt = sb("moe_gt", [P, EXPERTS])
        moe_n = sb("moe_n", [P, 1])
        moe_eq = sb("moe_eq", [P, EXPERTS])
        moe_cum = sb("moe_cum", [P, EXPERTS])
        moe_lt = sb("moe_lt", [P, EXPERTS])
        moe_both = sb("moe_both", [P, EXPERTS])
        moe_sel = sb("moe_sel", [P, EXPERTS])
        moe_c = sb("moe_c", [P, EXPERTS])
        acc = sb("acc", [P, 2, P])
        out_sb = sb("out_sb", [P, 2, P])
        scratch = nc.dram_tensor("qk_scratch", [2, 3 * PARTS - 1, P, P], BF16).ap()

        def after(eng, name, n):
            if isinstance(n, int) and n <= 0:
                return
            eng.wait_ge(S[name], n)

        def after_all(eng, *waits):
            waits = [(name, n) for name, n in waits if not isinstance(n, int) or n > 0]
            if any(not isinstance(n, int) for _, n in waits):
                for _, n in waits:
                    if not isinstance(n, int):
                        eng.lower_val(n)
                eng.wait_ge(S["const_pool"], 8)
            for name, n in waits:
                eng.wait_ge(S[name], n)

        def run(t, par, lag, piece, *more):
            k = t - lag
            if isinstance(t, int) and not 0 <= k < TILES:
                return
            piece(k, (par + lag) % 2, *more)

        def steps(eng, step, other_weights=None):
            for t in range(LOOP):
                step(t, t % 2)
                if t == 0 and other_weights:
                    other_weights()
            with eng.Fori(LOOP, TILES - 1, 2) as i:
                step(i, 0)
                step(i + 1, 1)
            for t in range(TILES, LAST):
                step(t, t % 2)

        def last_use(k, fill):
            users = USERS[BANK[fill]]
            me = [u[0] for u in users].index(fill)
            for back in range(1, len(users) + 1):
                n = me - back
                _, lag, name = users[n]
                other = k + users[me][1] - lag - (1 if n < 0 else 0)
                if not isinstance(other, int) or 0 <= other < TILES:
                    return name, other + 1
            return users[me][2], 0

        def bank_free(eng, k, fill):
            after(eng, *last_use(k, fill))

        block = stack.enter_context(nc.Block())

        @block.sync
        def _(sp):
            def load(dst, src, done):
                sp.dma_start(dst, src).then_inc(S[done], 16)

            def load_column(n, v, done):
                load(cols[:, n:n + 1], v.rearrange("(p a) -> p a", a=1), done)

            xr = x.rearrange("b s d -> s b d")
            load(x_all[:, 0:2, :], xr[:, 0:2, :], "x_first")
            load_column(0, w_mix, "w_col_a")
            for n, v in enumerate((Wg, Wv, Wd, Wo)):
                load(raw[:, R_GRU + n, :], v, "w_in_a")
            for n, v in enumerate((bg, bv, bd)):
                load_column(3 + n, v, "w_col_a")
            load_column(1, w_attn, "w_col_b")
            load(raw[:, R_QKV:R_QKV + 3, :], Wqkv.rearrange("(n p) k -> p n k", p=P), "w_in_q")
            load(raw[:, R_XWV, :], xWv, "w_in_q")
            load_column(2, w_ffn, "w_col_b")
            load(raw[:, R_GATE:R_GATE + FF, :], Wgate.rearrange("(n p) k -> p n k", p=P), "w_in_b")
            load(raw[:, R_UP:R_UP + FF, :], Wup.rearrange("(n p) k -> p n k", p=P), "w_in_b")
            load(raw[:, R_OUT:R_OUT + FF, :], Wout.rearrange("p (n k) -> p n k", k=P), "w_in_b")
            load(raw[:, R_WI:R_WI + EXPERTS, :], Wi.rearrange("e d h -> d e h"), "w_in_c")
            load(raw_xq[:], xWq, "w_in_c")
            load(raw_xk[:], xWk, "w_in_c")
            load(wmo_sb[:], Wmo.rearrange("e h d -> h e d"), "w_in_c")
            load(x_all[:, 2:TILES, :], xr[:, 2:TILES, :], "x_in")
            load(wr_sb[:], Wr, "w_small")
            load(mask_sb[:], mask, "w_small")
            load(xbv_sb[:], xbv.rearrange("(a n) -> a n", a=1).to_broadcast([P, P]), "w_small")

            def ctx_load(k, b):
                after_all(sp, ("ctx_T_ps", k))
                sp.dma_start(ctx_sb[:, b, :], ctx[k]).then_inc(S["ctx_in"], 16)

            def parts_save(k, b):
                after_all(sp, ("q_stacked", 16 * k))
                after_all(sp, ("qkv_hi", k + 1))
                after_all(sp, ("qkv_mid", k + 1))
                after_all(sp, ("qkv_lo", k + 1))
                sp.dma_start(scratch[b, 0:2 * PARTS].rearrange("c r s -> r c s"),
                             qk_parts[:, b].rearrange("p a c s -> p (a c) s")).then_inc(S["parts_saved"], 16)
                sp.dma_start(scratch[b, 2 * PARTS:3 * PARTS - 1].rearrange("c r s -> r c s"),
                             qk_parts[:, b, 1, 0:PARTS - 1]).then_inc(S["parts_saved"], 16)

            def parts_stack(k, b):
                after_all(sp, ("parts_saved", 32 * (k + 1)))
                after_all(sp, ("att_scores_ps", 4 * (k - 1)))
                after_all(sp, ("max_scores_ps", 4 * k))
                rot = scratch[b, PARTS:2 * PARTS]
                rot = bass.AP(rot.tensor, rot.offset, [[P * P, PARTS], [HEADS * P, PARTS * HD], [1, HEADS * P]])
                sp.dma_start(q_stack[0:QROWS, b, :, :], rot).then_inc(S["q_stacked"], 16)
                rep = scratch[b, 0:PARTS]
                rep = bass.AP(rep.tensor, rep.offset, [[0, PARTS], [HEADS * P, PARTS * HD], [1, HEADS * P]])
                sp.dma_start(k_stack[0:QROWS, b, :, :], rep).then_inc(S["k_stacked"], 16)

            def max_stack(k, b):
                after_all(sp, ("max_mT", k + 1))
                after_all(sp, ("att_scores_ps", 4 * k))
                sp.dma_start(q_stack[QROWS:SROWS, b, :, :], nmT[:, :]).then_inc(S["m_stacked"], 16)

            def store(k, b):
                after_all(sp, ("moe_out", k + 1))
                sp.dma_start(out[k], out_sb[:, b, :]).then_inc(S["stored"], 16)

            def step(t, par):
                run(t, par, 2, max_stack)
                run(t, par, 1, parts_save)
                run(t, par, 1, ctx_load)
                run(t, par, 5, store)
                run(t, par, 1, parts_stack)

            sp.wait_ge(S["const_dve"], 4)
            steps(sp, step)
            sp.wait_ge(S["stored"], 16 * TILES)

        @block.gpsimd
        def _(pool):
            nc.gpsimd.memset(ident[:], 0.0).then_inc(S["const_pool"], 1)
            pool.wait_ge(S["const_pool"], 1)
            nc.gpsimd.affine_select(out=ident[:], in_=ident[:], compare_op=ALU.not_equal, fill=1.0, base=0,
                                    pattern=[[-1, P]], channel_multiplier=1).then_inc(S["const_pool"], 1)
            nc.gpsimd.memset(above[:], 0.0).then_inc(S["const_pool"], 1)
            nc.gpsimd.memset(below[:], 0.0).then_inc(S["const_pool"], 1)
            nc.gpsimd.memset(neghalf[:], -0.5).then_inc(S["const_pool"], 1)
            pool.wait_ge(S["const_pool"], 5)
            nc.gpsimd.affine_select(out=above[:], in_=above[:], compare_op=ALU.is_ge, fill=MASKED, base=0,
                                    pattern=[[0, 4], [-1, P]], channel_multiplier=1).then_inc(S["const_pool"], 1)
            nc.gpsimd.affine_select(out=below[:], in_=below[:], compare_op=ALU.is_ge, fill=MASKED, base=0,
                                    pattern=[[0, 4], [1, P]], channel_multiplier=-1).then_inc(S["const_pool"], 1)
            pool.wait_ge(S["const_pool"], 7)
            nc.gpsimd.tensor_copy(identb[:], ident[:]).then_inc(S["const_pool"], 1)

            def power(src, dst, ready, n, mean, rsd, scale, eps, tmp, used):
                after_all(pool, (ready, n), (used, n - 1))
                nc.gpsimd.tensor_scalar(tmp, src, scale, eps, ALU.mult, ALU.add).then_inc(S[mean], 1)
                after(pool, mean, n)
                nc.gpsimd.tensor_tensor(dst, tmp, neghalf[:], ALU.pow).then_inc(S[rsd], 1)

            def gru_power(k, b):
                power(ss[:, 0:1], rs[:, 0:1], "gru_ss", k + 1, "gru_ms", "gru_rs", 1.0 / P, RMS_EPS, ms[:, 0:1], "gru_xn")

            def qkv_power(k, b):
                power(ss[:, 1:2], rs[:, 1:2], "qkv_ss", k + 1, "qkv_ms", "qkv_rs", 1.0 / P, RMS_EPS, ms[:, 1:2], "qkv_xn")

            def ffn_power(k, b):
                power(ss[:, 2:3], rs[:, 2:3], "ffn_ss", k + 1, "ffn_ms", "ffn_rs", 1.0 / P, RMS_EPS, ms[:, 2:3], "ffn_xn")

            def ffn_ln_power(k, b):
                power(mv[:, 0, 1:2], lrs[:, 0:1], "ffn_mv", k + 1, "ffn_ve", "ffn_rs1", 1.0, LN_EPS, ve[:, 0:1], "ffn_y1")

            def xat_ln_power(k, b):
                power(mv[:, 1, 1:2], lrs[:, 1:2], "xat_mv", k + 1, "xat_ve", "xat_rs", 1.0, LN_EPS, ve[:, 1:2], "xat_y2")

            def moe_ln_power(k, b):
                power(mv[:, 2, 1:2], lrs[:, 2:3], "moe_mv", k + 1, "moe_ve", "moe_rs", 1.0, LN_EPS, ve[:, 2:3], "moe_out")

            def gru_decay(k, b):
                after_all(pool, ("gru_tanh", k + 1), ("gru_scan", k))
                nc.gpsimd.tensor_scalar(gru_a[:], gru_t[:, 2, :], 0.499, 0.5, ALU.mult, ALU.add).then_inc(S["gru_decay"], 1)

            def ffn_residual(k, b):
                after(pool, "att_x2", k + 1)
                after(pool, "ffn_z", k)
                nc.gpsimd.tensor_tensor(x02[:], x_all[:, k, :], x2[:, b, :], ALU.add).then_inc(S["ffn_x02"], 1)

            def xat_residual(k, b):
                after(pool, "ffn_y1", k + 1)
                after(pool, "xat_z", k)
                nc.gpsimd.tensor_tensor(y1b[:], y1[:, b, :], xbv_sb[:], ALU.add).then_inc(S["xat_y1b"], 1)

            def max_split(k, b):
                after_all(pool, ("max_max", 4 * (k + 1)), ("max_mT_ps", k))
                nc.gpsimd.tensor_copy(nm_parts[:, 0, :], neg_max[:]).then_inc(S["max_n1"], 1)
                after(pool, "max_n1", k + 1)
                nc.gpsimd.tensor_tensor(nm_rest[:], neg_max[:], nm_parts[:, 0, :], ALU.subtract).then_inc(S["max_r1"], 1)
                after_all(pool, ("max_r1", k + 1))
                nc.gpsimd.tensor_copy(nm_parts[:, 1, :], nm_rest[:]).then_inc(S["max_n2"], 1)
                after(pool, "max_n2", k + 1)
                nc.gpsimd.tensor_tensor(nm_parts[:, 2, :], nm_rest[:], nm_parts[:, 1, :], ALU.subtract).then_inc(S["max_n3"], 1)

            def qk_low(k, b):
                after(pool, "qkv_mid", k + 1)
                after(pool, "parts_saved", 32 * (k - 1))
                nc.gpsimd.tensor_tensor(qk_parts[:, b, :, 2, :], qk_rest[:], qk_parts[:, b, :, 1, :], ALU.subtract).then_inc(S["qkv_lo"], 1)

            def step(t, par):
                run(t, par, 5, xat_ln_power)
                run(t, par, 0, gru_power)
                run(t, par, 2, qk_low)
                run(t, par, 1, gru_decay)
                run(t, par, 4, ffn_ln_power)
                run(t, par, 1, qkv_power)
                run(t, par, 4, xat_residual)
                run(t, par, 3, ffn_residual)
                run(t, par, 3, ffn_power)
                run(t, par, 5, moe_ln_power)
                run(t, par, 2, max_split)

            steps(pool, step)

        @block.tensor
        def _(pe):
            homes = [ps_scores, ps_probs]

            def turn_weights(g):
                for n in range(4):
                    last = nc.tensor.transpose(homes[g % 2][:, n, :], raw[:, 4 * g + n, :], ident[:])
                last.then_inc(S["w_ps"], 1)

            pe.wait_ge(S["const_pool"], 2)
            pe.wait_ge(S["w_in_a"], 64)
            turn_weights(0)
            pe.wait_ge(S["w_in_q"], 32)
            turn_weights(1)
            pe.wait_ge(S["w_dve"], 6)

            def other_weights():
                pe.wait_ge(S["const_pool"], 8)
                pe.wait_ge(S["w_in_b"], 48)
                turn_weights(2)
                turn_weights(3)
                pe.wait_ge(S["w_act"], 1)
                turn_weights(4)
                pe.wait_ge(S["w_in_c"], 64)
                pe.wait_ge(S["w_dve"], 7)
                turn_weights(5)
                pe.wait_ge(S["w_act"], 2)
                turn_weights(6)
                pe.wait_ge(S["w_dve"], 8)
                nc.tensor.matmul(ps_probs[:, 0, :], raw_xk[:], raw_xq[:], start=True, stop=True).then_inc(S["w_ps"], 1)
                pe.wait_ge(S["w_act"], 3)
                for g in range(2):
                    if g == 1:
                        pe.wait_ge(S["w_dve"], 9)
                    for n in range(4):
                        last = nc.tensor.matmul(homes[g][:, n, :], wiT[:, 4 * g + n, :], wmo_sb[:, 4 * g + n, :],
                                                start=True, stop=True)
                    last.then_inc(S["w_ps"], 1)
                pe.wait_ge(S["w_act"], 4)
                pe.wait_ge(S["w_dve"], 10)

            def turn(fill, k, src, done):
                bank_free(pe, k, fill)
                nc.tensor.transpose(view(fill)[:, 0, :], src, ident[:]).then_inc(S[done], 1)

            def gru_turn(k, b):
                after(pe, "gru_xn", k + 1)
                turn("gru_turn", k, xn[:, 0, :], "gru_xT_ps")

            def gru_gates(k, b):
                after(pe, "gru_xT", k + 1)
                bank_free(pe, k, "gru_gates")
                for n in range(3):
                    last = nc.tensor.matmul(view("gru_gates")[:, n, :], gruT[:, n, :], xT[:, 0, :], start=True, stop=True)
                last.then_inc(S["gru_gates_ps"], 1)

            def gru_turn_back(k, b):
                after(pe, "gru_scan", k + 1)
                turn("gru_turn_back", k, gru_h[:], "gru_hT_ps")

            def qkv_turn(k, b):
                after(pe, "qkv_xn", k + 1)
                turn("qkv_turn", k, xn[:, 1, :], "qkv_xT_ps")

            def qk_project(k, b):
                after(pe, "qkv_xT", k + 1)
                bank_free(pe, k, "qk_project")
                for n in range(2):
                    last = nc.tensor.matmul(view("qk_project")[:, n, :], qkvT[:, n, :], qkv_xT[:, b, :], start=True, stop=True)
                last.then_inc(S["qkv_ps"], 1)

            def v_project(k, b):
                after(pe, "qkv_xT", k + 1)
                bank_free(pe, k, "v_project")
                nc.tensor.matmul(view("v_project")[:, 0, :], qkv_xT[:, b, :], qkvT[:, 2, :], start=True, stop=True).then_inc(S["max_v_ps"], 1)

            def scores(k, b, n):
                if n == 0:
                    after(pe, "q_stacked", 16 * (k + 1))
                    after(pe, "k_stacked", 16 * (k + 1))
                after(pe, "max_max", 4 * k + n)
                for h in range(QUARTER):
                    nc.tensor.matmul(ps_scores[:, h, :], q_stack[0:QROWS, b, QUARTER * n + h, :],
                                     k_stack[0:QROWS, b, QUARTER * n + h, :], start=(h == 0), stop=False)
                nc.tensor.matmul(ps_scores[:], identb[:], above[:], start=False, stop=True).then_inc(S["max_scores_ps"], 1)

            def max_turn(k, b):
                after_all(pe, ("max_n3", k + 1), last_use(k, "max_turn"))
                nc.tensor.transpose(view("max_turn")[0:PARTS * HEADS, 0, 0:P // 2].bitcast(BF16),
                                    nm_parts[:].rearrange("p c h -> p (c h)"), identb[:]).then_inc(S["max_mT_ps"], 1)

            def scores_turned(k, b, n):
                if n == 0:
                    after(pe, "m_stacked", 16 * (k + 1))
                after(pe, "att_p", 4 * k + n)
                for h in range(QUARTER):
                    nc.tensor.matmul(ps_probs[:, h, :], k_stack[0:SROWS, b, QUARTER * n + h, :],
                                     q_stack[0:SROWS, b, QUARTER * n + h, :], start=(h == 0), stop=False)
                nc.tensor.matmul(ps_probs[:], identb[:], below[:], start=False, stop=True).then_inc(S["att_scores_ps"], 1)

            def att_values(k, b, n):
                if n == 0:
                    after(pe, "max_v", k + 1)
                    bank_free(pe, k, "att_values")
                after(pe, "att_p", 4 * k + n + 1)
                for h in range(QUARTER * n, QUARTER * n + QUARTER):
                    last = nc.tensor.matmul(o_view()[:, h, :], probs[:, n, h % QUARTER, :],
                                            values[:, b, h, :], start=True, stop=True)
                last.then_inc(S["att_o_ps"], 1)

            def att_turn(k, b):
                after(pe, "att_o", k + 1)
                turn("att_turn", k, att_o[:], "att_oT_ps")

            def att_project(k, b):
                after(pe, "att_oT", k + 1)
                bank_free(pe, k, "att_project")
                nc.tensor.matmul(view("att_project")[:, 0, :], att_oT[:], woT[:], start=True, stop=True).then_inc(S["att_y_ps"], 1)

            def ffn_turn(k, b):
                after(pe, "ffn_xn", k + 1)
                turn("ffn_turn", k, xn[:, 2, :], "ffn_xT_ps")

            def ffn_hidden(k, b, fill, g, done):
                after(pe, "ffn_xT", k + 1)
                bank_free(pe, k, fill)
                for n in range(FF):
                    last = nc.tensor.matmul(view(fill)[:, n, :], guT[:, g, n * P:(n + 1) * P], xT[:, 1, :], start=True, stop=True)
                last.then_inc(S[done], 1)

            def ffn_gate(k, b):
                ffn_hidden(k, b, "ffn_gate", 0, "ffn_gate_ps")

            def ffn_up(k, b):
                ffn_hidden(k, b, "ffn_up", 1, "ffn_up_ps")

            def ffn_down(k, b):
                after(pe, "ffn_h", k + 1)
                bank_free(pe, k, "ffn_down")
                for n in range(FF):
                    last = nc.tensor.matmul(view("ffn_down")[:, 0, :], hidden[:, n, :], outT[:, n, :], start=(n == 0), stop=(n == FF - 1))
                last.then_inc(S["ffn_y_ps"], 1)

            def ctx_turn(k, b):
                after(pe, "ctx_in", 16 * (k + 1))
                turn("ctx_turn", k, ctx_sb[:, b, :], "ctx_T_ps")

            def ctx_project(k, b):
                after(pe, "ctx_T", k + 1)
                bank_free(pe, k, "ctx_project")
                nc.tensor.matmul(view("ctx_project")[:, 0, :], w_kq[:], ctxT[:], start=True, stop=True)
                nc.tensor.matmul(view("ctx_project")[:, 1, :], ctxT[:], xwvT[:], start=True, stop=True).then_inc(S["ctx_kv_ps"], 1)

            def xat_turn(k, b):
                after(pe, "ffn_y1", k + 1)
                turn("xat_turn", k, y1[:, b, :], "xat_xT_ps")

            def xat_scores(k, b):
                if isinstance(k, int) and k == 0:
                    pe.wait_ge(S["w_small"], 48)
                after(pe, "xat_xT", k + 1)
                after(pe, "ctx_kv", k + 1)
                bank_free(pe, k, "xat_scores")
                nc.tensor.matmul(view("xat_scores")[:, 0, :], y1T[:], ctx_kv[:, b, 0, :], start=True, stop=True).then_inc(S["xat_s_ps"], 1)

            def xat_turn_probs(k, b):
                after(pe, "xat_p", k + 1)
                turn("xat_turn_probs", k, xat_p[:], "xat_pT_ps")

            def xat_values(k, b):
                after(pe, "xat_pT", k + 1)
                bank_free(pe, k, "xat_values")
                nc.tensor.matmul(view("xat_values")[:, 0, :], xat_pT[:], ctx_kv[:, b, 1, :], start=True, stop=True).then_inc(S["xat_y_ps"], 1)

            def moe_turn(k, b):
                after(pe, "xat_y2", k + 1)
                turn("moe_turn", k, y2[:, b, :], "moe_xT_ps")

            def moe_logits(k, b):
                after(pe, "moe_xT", k + 1)
                bank_free(pe, k, "moe_logits")
                nc.tensor.matmul(view("moe_logits")[:, 0, 0:EXPERTS], y2T[:], wr_sb[:], start=True, stop=True).then_inc(S["moe_logits_ps"], 1)

            def moe_experts(k, b, n):
                fill = ("moe_experts_0", "moe_experts_1")[n]
                after(pe, "moe_xT", k + 1)
                bank_free(pe, k, fill)
                nc.tensor.matmul(as_one(view(fill)), y2T[:], w_moe[:, 4 * n:4 * n + 4, :], start=True, stop=True).then_inc(S[("moe_m0_ps", "moe_m1_ps")[n]], 1)

            def step(t, par):
                run(t, par, 4, scores_turned, 3)
                run(t, par, 4, att_values, 2)
                run(t, par, 3, scores, 0)
                run(t, par, 4, att_values, 3)
                run(t, par, 5, xat_turn)
                run(t, par, 3, ctx_turn)
                run(t, par, 3, scores, 1)
                run(t, par, 2, qkv_turn)
                run(t, par, 4, att_turn)
                run(t, par, 5, xat_scores)
                run(t, par, 4, att_project)
                run(t, par, 3, scores, 2)
                run(t, par, 2, qk_project)
                run(t, par, 5, xat_turn_probs)
                run(t, par, 3, scores, 3)
                run(t, par, 5, xat_values)
                run(t, par, 4, ffn_turn)
                run(t, par, 1, gru_turn)
                run(t, par, 4, ffn_gate)
                run(t, par, 3, max_turn)
                run(t, par, 2, v_project)
                run(t, par, 3, ctx_project)
                run(t, par, 1, gru_gates)
                run(t, par, 5, moe_turn)
                run(t, par, 4, ffn_up)
                run(t, par, 5, moe_logits)
                run(t, par, 5, moe_experts, 0)
                run(t, par, 3, scores_turned, 0)
                run(t, par, 4, ffn_down)
                run(t, par, 1, gru_turn_back)
                run(t, par, 3, scores_turned, 1)
                run(t, par, 3, att_values, 0)
                run(t, par, 3, scores_turned, 2)
                run(t, par, 3, att_values, 1)
                run(t, par, 5, moe_experts, 1)

            steps(pe, step, other_weights)

        @block.scalar
        def _(act):
            act.wait_ge(S["const_pool"], 2)
            nc.scalar.activation(unused[:], ident[:, 0:1], ACT.Tanh)

            def other_weights():
                act.wait_ge(S["w_col_b"], 32)
                act.wait_ge(S["w_ps"], 3)
                nc.scalar.activation(guT[:, 0, :], as_one(ps_scores[:]), ACT.Copy, scale=cols[:, 2:3]).then_inc(S["w_act"], 1)
                act.wait_ge(S["w_ps"], 5)
                nc.scalar.activation(outT[:], ps_scores[:], ACT.Copy, scale=0.5).then_inc(S["w_act"], 1)
                act.wait_ge(S["w_ps"], 7)
                nc.scalar.copy(wiT[:, 4:8, :], ps_scores[:]).then_inc(S["w_act"], 1)
                act.wait_ge(S["w_ps"], 9)
                nc.scalar.copy(w_moe[:, 0:4, :], ps_scores[:]).then_inc(S["w_act"], 1)

            def squares(src, n, done):
                nc.scalar.activation(junk[:, n, :], src, ACT.Square, accum_out=ss[:, n:n + 1]).then_inc(S[done], 1)

            def normalize(k, src, n, rsd, done, used):
                after_all(act, (rsd, k + 1), (used, k))
                nc.scalar.activation(xn[:, n, :], src, ACT.Copy, scale=rs[:, n:n + 1]).then_inc(S[done], 1)

            def gru_squares(k, b):
                after_all(act, ("gru_ms", k))
                if isinstance(k, int) and k == 2:
                    act.wait_ge(S["x_in"], 16)
                squares(x_all[:, k, :], 0, "gru_ss")

            def gru_normalize(k, b):
                normalize(k, x_all[:, k, :], 0, "gru_rs", "gru_xn", "gru_xT_ps")

            def gru_copy(k, b):
                after(act, "gru_xT_ps", k + 1)
                after(act, "gru_gates_ps", k)
                nc.scalar.copy(xT[:, 0, :], view("gru_turn")[:, 0, :]).then_inc(S["gru_xT"], 1)

            def gru_tanh(k, b):
                after(act, "gru_gates_ps", k + 1)
                after(act, "gru_xs", k)
                after(act, "gru_decay", k)
                gates = view("gru_gates")
                nc.scalar.activation(gru_t[:, 0, :], gates[:, 0, :], ACT.Tanh, bias=half_b[:, 0:1], scale=0.5)
                nc.scalar.activation(gru_t[:, 1, :], gates[:, 1, :], ACT.Tanh, bias=cols[:, 4:5])
                nc.scalar.activation(gru_t[:, 2, :], gates[:, 2, :], ACT.Tanh, bias=half_b[:, 1:2], scale=0.5).then_inc(S["gru_tanh"], 1)

            def qkv_squares(k, b):
                after_all(act, ("gru_x1", k + 1), ("qkv_ms", k))
                squares(x1_all[:, k, :], 1, "qkv_ss")

            def qkv_normalize(k, b):
                normalize(k, x1_all[:, k, :], 1, "qkv_rs", "qkv_xn", "qkv_xT_ps")

            def qkv_copy(k, b):
                after(act, "qkv_xT_ps", k + 1)
                after(act, "max_v_ps", k - 1)
                after(act, "qkv_ps", k - 1)
                nc.scalar.copy(qkv_xT[:, b, :], view("qkv_turn")[:, 0, :]).then_inc(S["qkv_xT"], 1)

            def qk_high(k, b):
                after(act, "qkv_ps", k + 1)
                after(act, "parts_saved", 32 * (k - 1))
                nc.scalar.copy(qk_parts[:, b, :, 0, :], view("qk_project")[:, 0:2, :]).then_inc(S["qkv_hi"], 1)

            def qk_middle(k, b):
                after(act, "qkv_rest", k + 1)
                nc.scalar.copy(qk_parts[:, b, :, 1, :], qk_rest[:]).then_inc(S["qkv_mid"], 1)

            def v_copy(k, b):
                after(act, "max_v_ps", k + 1)
                after(act, "att_o_ps", 4 * (k - 1))
                nc.scalar.copy(values[:, b, :, 0:HD], view("v_project")[:, 0, :].rearrange("p (h d) -> p h d", h=HEADS)).then_inc(S["max_v"], 1)

            def max_copy(k, b):
                after(act, "max_mT_ps", k + 1)
                after(act, "m_stacked", 16 * k)
                nc.scalar.copy(nmT[:], view("max_turn")[0:PARTS * HEADS, 0, 0:P // 2].bitcast(BF16)).then_inc(S["max_mT"], 1)

            def exponentials(k, b, n):
                after(act, "att_scores_ps", 4 * k + n + 1)
                after(act, "att_o_ps", 4 * k + n - 3)
                nc.scalar.activation(probs[:, n, :, :], ps_probs[:], ACT.Exp, scale=HD ** -0.5).then_inc(S["att_p"], 1)

            def att_copy(k, b):
                after(act, "att_oT_ps", k + 1)
                after(act, "att_y_ps", k)
                nc.scalar.copy(att_oT[:], view("att_turn")[:, 0, :]).then_inc(S["att_oT"], 1)

            def ffn_squares(k, b):
                after(act, "att_x2", k + 1)
                after(act, "ffn_ms", k)
                squares(x2[:, b, :], 2, "ffn_ss")

            def ffn_normalize(k, b):
                normalize(k, x2[:, b, :], 2, "ffn_rs", "ffn_xn", "ffn_xT_ps")

            def ffn_copy(k, b):
                after(act, "ffn_xT_ps", k + 1)
                after(act, "ffn_gate_ps", k)
                after(act, "ffn_up_ps", k)
                nc.scalar.copy(xT[:, 1, :], view("ffn_turn")[:, 0, :]).then_inc(S["ffn_xT"], 1)

            def ffn_tanh(k, b):
                after(act, "ffn_gate_ps", k + 1)
                after(act, "ffn_t1", k)
                nc.scalar.activation(gate_t[:], as_one(view("ffn_gate")), ACT.Tanh, scale=0.5).then_inc(S["ffn_tanh"], 1)

            def ctx_copy(k, b):
                after(act, "ctx_T_ps", k + 1)
                after(act, "ctx_kv_ps", k)
                nc.scalar.copy(ctxT[:], view("ctx_turn")[:, 0, :]).then_inc(S["ctx_T"], 1)

            def ctx_copy_kv(k, b):
                after(act, "ctx_kv_ps", k + 1)
                after(act, "xat_y_ps", k - 1)
                nc.scalar.copy(ctx_kv[:, b, :, :], view("ctx_project")[:, 0:2, :]).then_inc(S["ctx_kv"], 1)

            def xat_copy(k, b):
                after(act, "xat_xT_ps", k + 1)
                after(act, "xat_s_ps", k)
                nc.scalar.copy(y1T[:], view("xat_turn")[:, 0, :]).then_inc(S["xat_xT"], 1)

            def xat_exp(k, b):
                after(act, "xat_negm", k + 1)
                after(act, "xat_pT_ps", k)
                after(act, "xat_rd", k)
                nc.scalar.activation(xat_p[:], xat_s[:], ACT.Exp, bias=xat_m[:, 1:2],
                                     accum_out=xat_l[:, 0:1]).then_inc(S["xat_p"], 1)

            def xat_copy_probs(k, b):
                after(act, "xat_pT_ps", k + 1)
                after(act, "xat_y_ps", k)
                nc.scalar.copy(xat_pT[:], view("xat_turn_probs")[:, 0, :]).then_inc(S["xat_pT"], 1)

            def moe_copy(k, b):
                after(act, "moe_xT_ps", k + 1)
                after(act, "moe_logits_ps", k)
                after(act, "moe_m0_ps", k)
                after(act, "moe_m1_ps", k)
                nc.scalar.copy(y2T[:], view("moe_turn")[:, 0, :]).then_inc(S["moe_xT"], 1)

            def moe_copy_logits(k, b):
                after(act, "moe_logits_ps", k + 1)
                after(act, "moe_c", k)
                nc.scalar.copy(moe_lg[:], view("moe_logits")[:, 0, 0:EXPERTS]).then_inc(S["moe_lg"], 1)

            def moe_exp(k, b):
                after(act, "moe_negm", k + 1)
                after(act, "moe_c", k)
                nc.scalar.activation(moe_e[:], moe_lg[:], ACT.Exp, bias=moe_m[:, 0:1],
                                     accum_out=moe_l[:, 0:1]).then_inc(S["moe_e"], 1)

            def step(t, par):
                run(t, par, 6, xat_copy_probs)
                run(t, par, 5, ffn_normalize)
                run(t, par, 3, qk_high)
                run(t, par, 4, ctx_copy)
                run(t, par, 5, ffn_copy)
                run(t, par, 2, gru_copy)
                run(t, par, 3, qk_middle)
                run(t, par, 4, max_copy)
                run(t, par, 3, v_copy)
                run(t, par, 5, ffn_tanh)
                run(t, par, 6, moe_copy)
                run(t, par, 2, gru_tanh)
                run(t, par, 4, ctx_copy_kv)
                run(t, par, 6, moe_copy_logits)
                run(t, par, 4, exponentials, 0)
                run(t, par, 6, moe_exp)
                run(t, par, 0, gru_squares)
                run(t, par, 1, gru_normalize)
                run(t, par, 4, exponentials, 1)
                run(t, par, 4, exponentials, 2)
                run(t, par, 2, qkv_squares)
                run(t, par, 4, exponentials, 3)
                run(t, par, 2, qkv_normalize)
                run(t, par, 5, xat_copy)
                run(t, par, 2, qkv_copy)
                run(t, par, 4, att_copy)
                run(t, par, 5, xat_exp)
                run(t, par, 4, ffn_squares)

            act.wait_ge(S["const_dve"], 4)
            act.wait_ge(S["w_col_a"], 64)
            act.wait_ge(S["x_first"], 16)
            steps(act, step, other_weights)

        @block.vector
        def _(dve):
            nc.vector.memset(k_stack[:].rearrange("p b h s -> p (b h s)").bitcast(F32), TWO_ONES).then_inc(S["const_dve"], 1)
            nc.vector.memset(values[:], 1.0).then_inc(S["const_dve"], 1)
            nc.vector.memset(ones8[:], 1.0).then_inc(S["const_dve"], 1)
            dve.wait_ge(S["w_col_a"], 64)
            nc.vector.tensor_scalar(half_b[:, 0:1], cols[:, 3:4], 0.5, None, ALU.mult)
            nc.vector.tensor_scalar(half_b[:, 1:2], cols[:, 5:6], 0.5, None, ALU.mult).then_inc(S["const_dve"], 1)
            dve.wait_ge(S["w_ps"], 1)
            nc.vector.tensor_scalar(gruT[:], ps_scores[:, 0:3, :], cols[:, 0:1], None, ALU.mult).then_inc(S["w_dve"], 1)
            nc.vector.tensor_copy(woT[:], ps_scores[:, 3, :]).then_inc(S["w_dve"], 1)
            dve.wait_ge(S["w_ps"], 2)
            dve.wait_ge(S["w_col_b"], 32)
            for n in range(2):
                nc.vector.tensor_scalar(qkvT[:, n, :].rearrange("p (d h) -> p h d", d=HD),
                                        ps_probs[:, 1 - n, :].rearrange("p (h d) -> p h d", d=HD),
                                        cols[:, 1:2], None, ALU.mult).then_inc(S["w_dve"], 1)
            nc.vector.tensor_scalar(qkvT[:, 2, :], ps_probs[:, 2, :], cols[:, 1:2], None, ALU.mult).then_inc(S["w_dve"], 1)
            nc.vector.tensor_copy(xwvT[:], ps_probs[:, 3, :]).then_inc(S["w_dve"], 1)

            def other_weights():
                dve.wait_ge(S["w_ps"], 4)
                nc.vector.tensor_scalar(guT[:, 1, :], as_one(ps_probs[:]), cols[:, 2:3], None, ALU.mult).then_inc(S["w_dve"], 1)
                dve.wait_ge(S["w_ps"], 6)
                nc.vector.tensor_copy(wiT[:, 0:4, :], ps_probs[:]).then_inc(S["w_dve"], 1)
                dve.wait_ge(S["w_ps"], 8)
                nc.vector.tensor_scalar(w_kq[:], ps_probs[:, 0, :], P ** -0.5, None, ALU.mult).then_inc(S["w_dve"], 1)
                dve.wait_ge(S["w_ps"], 10)
                nc.vector.tensor_copy(w_moe[:, 4:8, :], ps_probs[:]).then_inc(S["w_dve"], 1)

            def layernorm_apply(n, k, src, dst, rsd, done):
                after(dve, rsd, k + 1)
                nc.vector.tensor_scalar(dst, src, mv[:, n, 0:1], lrs[:, n:n + 1], ALU.subtract, ALU.mult).then_inc(S[done], 1)

            def gru_input(k, b):
                after(dve, "gru_tanh", k + 1)
                after(dve, "gru_scan", k)
                nc.vector.scalar_tensor_tensor(gru_xs[:], gru_t[:, 0, :], 1.0, gru_t[:, 1, :], ALU.add, ALU.mult).then_inc(S["gru_xs"], 1)

            def gru_scan(k, b):
                after(dve, "gru_xs", k + 1)
                after(dve, "gru_decay", k + 1)
                after(dve, "gru_hT_ps", k)
                nc.vector.tensor_tensor_scan(gru_h[:], gru_a[:], gru_xs[:], 0.0, ALU.mult, ALU.add).then_inc(S["gru_scan"], 1)

            def gru_out(k, b):
                after(dve, "gru_hT_ps", k + 1)
                nc.vector.scalar_tensor_tensor(x1_all[:, k, :], view("gru_turn_back")[:, 0, :], 0.5, x_all[:, k, :],
                                               ALU.mult, ALU.add).then_inc(S["gru_x1"], 1)

            def qk_rest_of(k, b):
                after(dve, "qkv_hi", k + 1)
                after(dve, "qkv_lo", k)
                nc.vector.tensor_tensor(qk_rest[:], view("qk_project")[:, 0:2, :], qk_parts[:, b, :, 0, :],
                                        ALU.subtract).then_inc(S["qkv_rest"], 1)

            def maxima(k, b, n):
                after(dve, "max_scores_ps", 4 * k + n + 1)
                if n == 0:
                    after(dve, "max_n3", k)
                nc.vector.tensor_reduce(neg_max[:, QUARTER * n:QUARTER * n + QUARTER], ps_scores[:], AX_X,
                                        ALU.max, negate=True).then_inc(S["max_max"], 1)

            def att_reciprocal(k, b):
                after(dve, "att_o_ps", 4 * (k + 1))
                after(dve, "att_o", k)
                nc.vector.reciprocal(att_rd[:], o_view()[:, :, HD]).then_inc(S["att_rd"], 1)

            def att_divide(k, b):
                after(dve, "att_rd", k + 1)
                after(dve, "att_oT_ps", k)
                nc.vector.tensor_tensor(att_o[:].rearrange("p (h d) -> p h d", h=HEADS), o_view()[:, :, 0:HD],
                                        att_rd[:].unsqueeze(2).to_broadcast([P, HEADS, HD]), ALU.mult).then_inc(S["att_o"], 1)

            def att_out(k, b):
                after(dve, "att_y_ps", k + 1)
                after(dve, "ffn_x02", k - 1)
                after(dve, "ffn_xn", k - 1)
                nc.vector.tensor_tensor(x2[:, b, :], view("att_project")[:, 0, :], x1_all[:, k, :], ALU.add).then_inc(S["att_x2"], 1)

            def ffn_silu(k, b):
                after(dve, "ffn_tanh", k + 1)
                after(dve, "ffn_h", k)
                nc.vector.scalar_tensor_tensor(gate_1[:], gate_t[:], 1.0, as_one(view("ffn_gate")), ALU.add, ALU.mult).then_inc(S["ffn_t1"], 1)

            def ffn_product(k, b):
                after(dve, "ffn_t1", k + 1)
                after(dve, "ffn_up_ps", k + 1)
                after(dve, "ffn_y_ps", k)
                nc.vector.tensor_tensor(hidden[:].rearrange("p a b -> p (a b)"), gate_1[:], as_one(view("ffn_up")), ALU.mult).then_inc(S["ffn_h"], 1)

            def ffn_out(k, b):
                after(dve, "ffn_y_ps", k + 1)
                after(dve, "ffn_x02", k + 1)
                after(dve, "ffn_y1", k)
                nc.vector.tensor_tensor(z[:, 0, :], view("ffn_down")[:, 0, :], x02[:], ALU.add).then_inc(S["ffn_z"], 1)

            def ffn_stats(k, b):
                after(dve, "ffn_z", k + 1)
                after(dve, "ffn_mv", k)
                nc.vector.bn_stats(stats[:, 0, :], z[:, 0, :]).then_inc(S["ffn_stats"], 1)

            def ffn_moments(k, b):
                after_all(dve, ("ffn_stats", k + 1), ("ffn_y1", k))
                nc.vector.bn_aggr(mv[:, 0, :], stats[:, 0, :]).then_inc(S["ffn_mv"], 1)

            def ffn_layernorm(k, b):
                after(dve, "xat_xT_ps", k - 1)
                after(dve, "xat_y1b", k - 1)
                layernorm_apply(0, k, z[:, 0, :], y1[:, b, :], "ffn_rs1", "ffn_y1")

            def xat_add_mask(k, b):
                after_all(dve, ("xat_s_ps", k + 1), ("xat_p", k))
                nc.vector.tensor_tensor_reduce(xat_s[:], view("xat_scores")[:, 0, :], mask_sb[:], 1.0, -3.4e38, ALU.add,
                                               ALU.max, xat_m[:, 0:1]).then_inc(S["xat_sm"], 1)

            def xat_negate(k, b):
                after(dve, "xat_sm", k + 1)
                nc.vector.tensor_scalar(xat_m[:, 1:2], xat_m[:, 0:1], -1.0, None, ALU.mult).then_inc(S["xat_negm"], 1)

            def xat_reciprocal(k, b):
                after(dve, "xat_p", k + 1)
                after(dve, "xat_z", k)
                nc.vector.reciprocal(xat_l[:, 1:2], xat_l[:, 0:1]).then_inc(S["xat_rd"], 1)

            def xat_out(k, b):
                after(dve, "xat_rd", k + 1)
                after(dve, "xat_y_ps", k + 1)
                after(dve, "xat_y1b", k + 1)
                after(dve, "xat_y2", k)
                nc.vector.scalar_tensor_tensor(z[:, 1, :], view("xat_values")[:, 0, :], xat_l[:, 1:2], y1b[:],
                                               ALU.mult, ALU.add).then_inc(S["xat_z"], 1)

            def xat_stats(k, b):
                after(dve, "xat_z", k + 1)
                after(dve, "xat_mv", k)
                nc.vector.bn_stats(stats[:, 1, :], z[:, 1, :]).then_inc(S["xat_stats"], 1)

            def xat_moments(k, b):
                after_all(dve, ("xat_stats", k + 1), ("xat_y2", k))
                nc.vector.bn_aggr(mv[:, 1, :], stats[:, 1, :]).then_inc(S["xat_mv"], 1)

            def xat_layernorm(k, b):
                after(dve, "moe_xT_ps", k - 1)
                after(dve, "moe_low", k - 1)
                layernorm_apply(1, k, z[:, 1, :], y2[:, b, :], "xat_rs", "xat_y2")

            def moe_top(k, b):
                after_all(dve, ("moe_lg", k + 1), ("moe_c", k))
                nc.vector.max(top[:], moe_lg[:]).then_inc(S["moe_top"], 1)
                after(dve, "moe_top", k + 1)
                nc.vector.tensor_scalar(moe_m[:, 0:1], top[:, 0:1], -1.0, None, ALU.mult).then_inc(S["moe_negm"], 1)

            def moe_choose(k, b):
                after(dve, "moe_top", k + 1)
                after(dve, "moe_c", k)
                nc.vector.tensor_scalar(moe_eq[:], moe_lg[:], top[:, 1:2], None, ALU.is_equal).then_inc(S["moe_eq"], 1)
                nc.vector.tensor_scalar(moe_gt[:], moe_lg[:], top[:, 1:2], None, ALU.is_gt, ALU.add,
                                        accum_out=moe_n[:]).then_inc(S["moe_gt"], 1)
                after(dve, "moe_eq", k + 1)
                nc.vector.tensor_tensor_scan(moe_cum[:], ones8[:], moe_eq[:], 0.0, ALU.mult, ALU.add).then_inc(S["moe_cum"], 1)
                after(dve, "moe_cum", k + 1)
                after(dve, "moe_gt", k + 1)
                nc.vector.tensor_scalar(moe_lt[:], moe_cum[:], moe_n[:], 2.5, ALU.add, ALU.is_lt).then_inc(S["moe_lt"], 1)
                after(dve, "moe_lt", k + 1)
                nc.vector.tensor_tensor(moe_both[:], moe_lt[:], moe_eq[:], ALU.mult).then_inc(S["moe_both"], 1)
                after(dve, "moe_both", k + 1)
                nc.vector.tensor_tensor(moe_sel[:], moe_both[:], moe_gt[:], ALU.add).then_inc(S["moe_sel"], 1)

            def moe_weights(k, b):
                after(dve, "moe_e", k + 1)
                after(dve, "moe_z", k)
                nc.vector.reciprocal(moe_l[:, 1:2], moe_l[:, 0:1]).then_inc(S["moe_rd"], 1)
                after(dve, "moe_sel", k + 1)
                after(dve, "moe_rd", k + 1)
                nc.vector.scalar_tensor_tensor(moe_c[:], moe_sel[:], moe_l[:, 1:2], moe_e[:], ALU.mult, ALU.mult).then_inc(S["moe_c"], 1)

            def moe_mix(k, b, n):
                after(dve, ("moe_m0_ps", "moe_m1_ps")[n], k + 1)
                after(dve, ("moe_c", "moe_low")[n], k + 1)
                if n == 0:
                    after(dve, "moe_z", k)
                for e in range(4 * n, 4 * n + 4):
                    if e >= 2 and e != 5:
                        after(dve, "moe_acc", 6 * k + (0, 0, 1, 2, 3, 0, 4, 5)[e])
                    term = view(("moe_experts_0", "moe_experts_1")[n])[:, e % 4, :]
                    done = ("moe_low", "moe_high")[n] if e % 4 == 3 else "moe_acc"
                    if e == 1:
                        nc.vector.tensor_scalar(acc[:, 1, :], term, moe_c[:, 1:2], None, ALU.mult).then_inc(S[done], 1)
                    else:
                        nc.vector.scalar_tensor_tensor(acc[:, e % 2, :], term, moe_c[:, e:e + 1],
                                                       acc[:, e % 2, :] if e else y2[:, b, :], ALU.mult,
                                                       ALU.add).then_inc(S[done], 1)

            def moe_sum(k, b):
                after(dve, "moe_out", k)
                after(dve, "moe_high", k + 1)
                nc.vector.tensor_tensor(z[:, 2, :], acc[:, 0, :], acc[:, 1, :], ALU.add).then_inc(S["moe_z"], 1)

            def moe_stats(k, b):
                after(dve, "moe_z", k + 1)
                after(dve, "moe_mv", k)
                nc.vector.bn_stats(stats[:, 2, :], z[:, 2, :]).then_inc(S["moe_stats"], 1)

            def moe_moments(k, b):
                after_all(dve, ("moe_stats", k + 1), ("moe_out", k))
                nc.vector.bn_aggr(mv[:, 2, :], stats[:, 2, :]).then_inc(S["moe_mv"], 1)

            def moe_layernorm(k, b):
                after(dve, "stored", 16 * k)
                layernorm_apply(2, k, z[:, 2, :], out_sb[:, b, :], "moe_rs", "moe_out")

            def step(t, par):
                run(t, par, 2, gru_scan)
                run(t, par, 6, moe_choose)
                run(t, par, 5, ffn_out)
                run(t, par, 6, moe_weights)
                run(t, par, 5, ffn_stats)
                run(t, par, 2, gru_out)
                run(t, par, 5, ffn_moments)
                run(t, par, 6, moe_mix, 0)
                run(t, par, 5, ffn_layernorm)
                run(t, par, 6, moe_mix, 1)
                run(t, par, 3, maxima, 0)
                run(t, par, 4, att_reciprocal)
                run(t, par, 4, att_divide)
                run(t, par, 3, maxima, 1)
                run(t, par, 5, xat_add_mask)
                run(t, par, 5, xat_negate)
                run(t, par, 4, att_out)
                run(t, par, 6, moe_sum)
                run(t, par, 3, maxima, 2)
                run(t, par, 6, moe_stats)
                run(t, par, 6, moe_moments)
                run(t, par, 5, xat_reciprocal)
                run(t, par, 3, maxima, 3)
                run(t, par, 5, xat_out)
                run(t, par, 5, xat_stats)
                run(t, par, 2, qk_rest_of)
                run(t, par, 5, xat_moments)
                run(t, par, 6, moe_layernorm)
                run(t, par, 5, xat_layernorm)
                run(t, par, 4, ffn_silu)
                run(t, par, 4, ffn_product)
                run(t, par, 1, gru_input)
                run(t, par, 5, moe_top)

            dve.wait_ge(S["x_first"], 16)
            steps(dve, step, other_weights)


_INS = ['x', 'ctx_1024', 'mask_SxS2_fk0', 'L0_attn_w_rms_mix', 'L0_attn_Wg', 'L0_attn_bg', 'L0_attn_Wv',
        'L0_attn_bv', 'L0_attn_Wd', 'L0_attn_bd', 'L0_attn_w_rms_attn', 'L0_attn_Wqkv', 'L0_attn_Wo',
        'L0_attn_w_rms_ffn', 'L0_attn_Wgate', 'L0_attn_Wup', 'L0_attn_Wout', 'L0_xattn_Wq', 'L0_xattn_Wk',
        'L0_xattn_Wv', 'L0_xattn_bv', 'L0_ffn_Wr', 'L0_ffn_Wi', 'L0_ffn_Wo']


def kernel(**inputs):
    import numpy as _np
    import concourse.bacc as _bacc
    from concourse import mybir as _mybir
    from concourse.bass_utils import run_bass_kernel_spmd as _run

    nc = _bacc.Bacc("TRN2", target_bir_lowering=False, num_devices=1)
    arrays, args = {}, []
    for name in _INS:
        a = _np.ascontiguousarray(inputs[name])
        arrays[f"in_{name}_dram"] = a
        args.append(nc.dram_tensor(f"in_{name}_dram", a.shape, _mybir.dt.from_np(a.dtype), kind="ExternalInput").ap())
    shape = inputs["x"].shape
    args.append(nc.dram_tensor("out_0_dram", shape, _mybir.dt.float32, kind="ExternalOutput").ap())
    decoder_layer(nc, *args)
    r = _run(nc, [arrays], core_ids=[0])
    return r.results[0]["out_0_dram"]
```
